# Optimizing a Trainium2 kernel written in Bass

```python
import numpy as np
import jax
import jax.numpy as jnp

def _softmax(x, axis=-1):
    return jax.nn.softmax(x, axis=axis)

def _gelu(x):
    return jax.nn.gelu(x, approximate=True)

def _silu(x):
    return jax.nn.silu(x)

def _sigmoid(x):
    return jax.nn.sigmoid(x)

def _layernorm(x, axis=-1, eps=1e-05):
    m = jnp.mean(x, axis=axis, keepdims=True)
    v = jnp.var(x, axis=axis, keepdims=True)
    return (x - m) / jnp.sqrt(v + eps)

def _scatter_add(tgt, idx, src, axis=0):
    return tgt.at[idx].add(src)

def _segment_sum(src, seg, n):
    return jax.ops.segment_sum(src, seg, n)
kernel_name = 'mk_cond_seq_d4_seqx_r8_df0d8f'

def setup_inputs(seed: int=0):
    np.random.seed(seed)
    _w = jnp.asarray

    def _rec_inputs():
        import jax
        import jax.numpy as jnp
        _rk = jax.random.key(seed)
        x = 7.22e-05 + 1 * jax.random.normal(jax.random.fold_in(_rk, 1), (8, 128, 128), jnp.float32)
        _lenS = 128 - jax.random.randint(jax.random.fold_in(_rk, 7), (8,), 0, max(1, 128 // 4) + 1, jnp.int32)
        _lenS2 = 128 - jax.random.randint(jax.random.fold_in(_rk, 8), (8,), 0, max(1, 128 // 4) + 1, jnp.int32)
        cond_1024 = 0.0061147 + 1.02565 * jax.random.normal(jax.random.fold_in(_rk, 11), (8, 128), jnp.float32)
        _validS = jnp.arange(128)[None, :] < _lenS[:, None]
        _validS2 = jnp.arange(128)[None, :] < _lenS2[:, None]
        _causal = jnp.tril(jnp.ones((128, 128), dtype=bool))
        mask_BxS_ik0 = jnp.where(jnp.broadcast_to(_validS[:, :], (8, 128)), 0, 1).astype(jnp.int32)
        return (x, cond_1024, mask_BxS_ik0)
    x, cond_1024, mask_BxS_ik0 = _rec_inputs()

    def _L0_cond_setup():
        import jax, jax.numpy as jnp
        import numpy as np
        D = 128
        H = 16
        HKV = 4
        HD = D // H
        REP = H // HKV
        DFF = 512
        B, N = (4, 256)
        EPS = 1e-05
        WSCALE = 0.02

        def _ln(x):
            m = jnp.mean(x, axis=-1, keepdims=True)
            v = jnp.mean(jnp.square(x - m), axis=-1, keepdims=True)
            return (x - m) * jax.lax.rsqrt(v + EPS)

        def _gqa_attn(h, wq, wk, wv, wo):
            b, n, d = h.shape
            q = (h @ wq.T).reshape(b, n, HKV, REP, HD)
            k = (h @ wk.T).reshape(b, n, HKV, HD)
            v = (h @ wv.T).reshape(b, n, HKV, HD)
            scores = jnp.einsum('bqgrh,bkgh->bgrqk', q, k) * (1.0 / np.sqrt(HD))
            a = jax.nn.softmax(scores, axis=-1)
            out = jnp.einsum('bgrqk,bkgh->bqgrh', a, v).reshape(b, n, d)
            return out @ wo.T

        def _mlp(h, w1, b1, w2, b2):
            h = jax.nn.gelu(h @ w1.T + b1, approximate=False)
            return h @ w2.T + b2
        key = jax.random.key(seed)
        ks = jax.random.split(key, 10)
        return {'x': jax.random.normal(ks[0], (B, N, D), jnp.float32), 'c': jax.random.normal(ks[1], (B, D), jnp.float32), 'wq': jax.random.normal(ks[2], (D, D), jnp.float32) * WSCALE, 'wk': jax.random.normal(ks[3], (HKV * HD, D), jnp.float32) * WSCALE, 'wv': jax.random.normal(ks[4], (HKV * HD, D), jnp.float32) * WSCALE, 'wo': jax.random.normal(ks[5], (D, D), jnp.float32) * WSCALE, 'w1': jax.random.normal(ks[6], (DFF, D), jnp.float32) * WSCALE, 'b1': jnp.zeros((DFF,), jnp.float32), 'w2': jax.random.normal(ks[7], (D, DFF), jnp.float32) * WSCALE, 'b2': jnp.zeros((D,), jnp.float32), 'wc': jax.random.normal(ks[8], (6 * D, D), jnp.float32) * WSCALE, 'bc': jnp.zeros((6 * D,), jnp.float32)}
    _L0_cond_all = _L0_cond_setup()
    _L0_cond_in = {k: v for k, v in _L0_cond_all.items() if k in ('wq', 'wk', 'wv', 'wo', 'w1', 'b1', 'w2', 'b2', 'wc', 'bc')}
    del _L0_cond_all

    def _L1_cond_setup():
        import jax, jax.numpy as jnp
        import numpy as np
        H = 16
        EPS = 1e-05

        def layer_norm(x, g, b):
            mu = jnp.mean(x, axis=-1, keepdims=True)
            var = jnp.var(x, axis=-1, keepdims=True)
            return (x - mu) * jax.lax.rsqrt(var + EPS) * g + b
        key = jax.random.key(seed)
        ks = jax.random.split(key, 8)
        B, T, D, TE = (4, 512, 128, 128)
        s = 0.02
        return {'x': jax.random.normal(ks[0], (B, T, D), jnp.float32), 'emb': jax.random.normal(ks[1], (B, 1, TE), jnp.float32), 'gate_msa': jax.random.normal(ks[2], (B, 1, D), jnp.float32), 'norm_g': jnp.ones((D,), jnp.float32), 'norm_b': jnp.zeros((D,), jnp.float32), 'Wq': jax.random.normal(ks[3], (D, D), jnp.float32) * s, 'bq': jnp.zeros((D,), jnp.float32), 'Wk': jax.random.normal(ks[4], (D, D), jnp.float32) * s, 'bk': jnp.zeros((D,), jnp.float32), 'Wv': jax.random.normal(ks[5], (D, D), jnp.float32) * s, 'bv': jnp.zeros((D,), jnp.float32), 'emb_W': jax.random.normal(ks[6], (TE, 2 * D), jnp.float32) * s, 'emb_b': jnp.zeros((2 * D,), jnp.float32), 'sn_g': jnp.ones((D,), jnp.float32), 'sn_b': jnp.zeros((D,), jnp.float32), 'out_W': jax.random.normal(ks[7], (D, D), jnp.float32) * s, 'out_b': jnp.zeros((D,), jnp.float32)}
    _L1_cond_all = _L1_cond_setup()
    _L1_cond_in = {k: v for k, v in _L1_cond_all.items() if k in ('norm_g', 'norm_b', 'Wq', 'bq', 'Wk', 'bk', 'Wv', 'bv', 'emb_W', 'emb_b', 'sn_g', 'sn_b', 'out_W', 'out_b')}
    del _L1_cond_all

    def _L2_cond_setup():
        import math
        import jax, jax.numpy as jnp
        import numpy as np
        D_MODEL = 128
        N_HEADS = 16
        FFN_DIM = 512
        EPS = 1e-05

        def _layernorm(x, w, b):
            mu = jnp.mean(x, axis=-1, keepdims=True)
            var = jnp.var(x, axis=-1, keepdims=True)
            return (x - mu) * jax.lax.rsqrt(var + EPS) * w + b

        def _modulate(x, shift, scale):
            return x * (1.0 + scale[:, None, :]) + shift[:, None, :]
        key = jax.random.key(seed)
        ks = jax.random.split(key, 16)
        B, S, D, F = (2, 256, D_MODEL, FFN_DIM)
        s = 0.02
        return {'x': jax.random.normal(ks[0], (B, S, D), jnp.float32), 't_emb': jax.random.normal(ks[1], (B, D), jnp.float32), 'ln1_w': jnp.ones((D,), jnp.float32), 'ln1_b': jnp.zeros((D,), jnp.float32), 'ln2_w': jnp.ones((D,), jnp.float32), 'ln2_b': jnp.zeros((D,), jnp.float32), 'wq': jax.random.normal(ks[2], (D, D), jnp.float32) * s, 'bq': jnp.zeros((D,), jnp.float32), 'wk': jax.random.normal(ks[3], (D, D), jnp.float32) * s, 'bk': jnp.zeros((D,), jnp.float32), 'wv': jax.random.normal(ks[4], (D, D), jnp.float32) * s, 'bv': jnp.zeros((D,), jnp.float32), 'wo': jax.random.normal(ks[5], (D, D), jnp.float32) * s, 'bo': jnp.zeros((D,), jnp.float32), 'wt_attn': jax.random.normal(ks[6], (D, 2 * D), jnp.float32) * s, 'bt_attn': jnp.zeros((2 * D,), jnp.float32), 'wt_ffn': jax.random.normal(ks[7], (D, 2 * D), jnp.float32) * s, 'bt_ffn': jnp.zeros((2 * D,), jnp.float32), 'w1': jax.random.normal(ks[8], (D, F), jnp.float32) * s, 'b1': jnp.zeros((F,), jnp.float32), 'w2': jax.random.normal(ks[9], (F, D), jnp.float32) * s, 'b2': jnp.zeros((D,), jnp.float32)}
    _L2_cond_all = _L2_cond_setup()
    _L2_cond_in = {k: v for k, v in _L2_cond_all.items() if k in ('ln1_w', 'ln1_b', 'ln2_w', 'ln2_b', 'wq', 'bq', 'wk', 'bk', 'wv', 'bv', 'wo', 'bo', 'wt_attn', 'bt_attn', 'wt_ffn', 'bt_ffn', 'w1', 'b1', 'w2', 'b2')}
    del _L2_cond_all

    def _L3_cond_setup():
        import jax, jax.numpy as jnp
        import numpy as np
        EMBED = 128
        HEADS = 16
        HEAD_DIM = EMBED // HEADS
        MLP = 4 * EMBED
        EPS = 1e-06

        def _adaln(x, c, norm_w, scale_w, scale_b, shift_w, shift_b):
            sc = jax.nn.silu(c)
            shift = sc @ shift_w.T + shift_b
            scale = jnp.clip(sc @ scale_w.T + scale_b + 1.0, 0.1, 10.0)
            norm = jnp.maximum(jnp.linalg.norm(x, axis=-1, keepdims=True) * x.shape[-1] ** (-0.5), EPS)
            h = x / norm * norm_w
            return h * scale[:, None, :] + shift[:, None, :]

        def _attention(x, attention_mask, qkv_w, proj_w, proj_b):
            B, N, C = x.shape
            qkv = (x @ qkv_w.T).reshape(B, N, 3, HEADS, HEAD_DIM)
            q = qkv[:, :, 0].transpose(0, 2, 1, 3)
            k = qkv[:, :, 1].transpose(0, 2, 1, 3)
            v = qkv[:, :, 2].transpose(0, 2, 1, 3)
            attn = jnp.einsum('bhnd,bhmd->bhnm', q, k) * HEAD_DIM ** (-0.5)
            mask = attention_mask[:, None, None, :]
            attn = jnp.where(mask == 0, -jnp.inf, attn)
            all_inf = jnp.all(attn == -jnp.inf, axis=-1, keepdims=True)
            attn = jnp.where(all_inf, 0.0, attn)
            p = jax.nn.softmax(attn, axis=-1)
            out = jnp.einsum('bhnm,bhmd->bhnd', p, v).transpose(0, 2, 1, 3).reshape(B, N, C)
            return out @ proj_w.T + proj_b

        def _mlp(x, w1, b1, w2, b2):
            h = x @ w1.T + b1
            x1, x2 = jnp.split(h, 2, axis=-1)
            return jax.nn.silu(x1) * x2 @ w2.T + b2
        key = jax.random.key(seed)
        ks = jax.random.split(key, 16)
        B, N, C = (2, 256, EMBED)
        x = jax.random.normal(ks[0], (B, N, C), dtype=jnp.float32)
        c = jax.random.normal(ks[1], (B, C), dtype=jnp.float32)
        attention_mask = jax.random.randint(ks[2], (B, N), 0, 2, dtype=jnp.int32)
        s = 0.02
        params = {'norm_w': jnp.ones((C,), jnp.float32), 'scale_w': s * jax.random.normal(ks[3], (C, C), jnp.float32), 'scale_b': s * jax.random.normal(ks[4], (C,), jnp.float32), 'shift_w': s * jax.random.normal(ks[5], (C, C), jnp.float32), 'shift_b': s * jax.random.normal(ks[6], (C,), jnp.float32), 'qkv_w': s * jax.random.normal(ks[7], (3 * C, C), jnp.float32), 'proj_w': s * jax.random.normal(ks[8], (C, C), jnp.float32), 'proj_b': s * jax.random.normal(ks[9], (C,), jnp.float32), 'mlp_w1': s * jax.random.normal(ks[10], (2 * MLP, C), jnp.float32), 'mlp_b1': s * jax.random.normal(ks[11], (2 * MLP,), jnp.float32), 'mlp_w2': s * jax.random.normal(ks[12], (C, MLP), jnp.float32), 'mlp_b2': s * jax.random.normal(ks[13], (C,), jnp.float32)}
        return {'x': x, 'c': c, 'attention_mask': attention_mask, **params}
    _L3_cond_all = _L3_cond_setup()
    _L3_cond_in = {k: v for k, v in _L3_cond_all.items() if k in ('norm_w', 'scale_w', 'scale_b', 'shift_w', 'shift_b', 'qkv_w', 'proj_w', 'proj_b', 'mlp_w1', 'mlp_b1', 'mlp_w2', 'mlp_b2')}
    del _L3_cond_all
    return {'x': x, 'cond_1024': cond_1024, 'mask_BxS_ik0': mask_BxS_ik0, 'L0_cond_wq': _L0_cond_in['wq'], 'L0_cond_wk': _L0_cond_in['wk'], 'L0_cond_wv': _L0_cond_in['wv'], 'L0_cond_wo': _L0_cond_in['wo'], 'L0_cond_w1': _L0_cond_in['w1'], 'L0_cond_b1': _L0_cond_in['b1'], 'L0_cond_w2': _L0_cond_in['w2'], 'L0_cond_b2': _L0_cond_in['b2'], 'L0_cond_wc': _L0_cond_in['wc'], 'L0_cond_bc': _L0_cond_in['bc'], 'L1_cond_norm_g': _L1_cond_in['norm_g'], 'L1_cond_norm_b': _L1_cond_in['norm_b'], 'L1_cond_Wq': _L1_cond_in['Wq'], 'L1_cond_bq': _L1_cond_in['bq'], 'L1_cond_Wk': _L1_cond_in['Wk'], 'L1_cond_bk': _L1_cond_in['bk'], 'L1_cond_Wv': _L1_cond_in['Wv'], 'L1_cond_bv': _L1_cond_in['bv'], 'L1_cond_emb_W': _L1_cond_in['emb_W'], 'L1_cond_emb_b': _L1_cond_in['emb_b'], 'L1_cond_sn_g': _L1_cond_in['sn_g'], 'L1_cond_sn_b': _L1_cond_in['sn_b'], 'L1_cond_out_W': _L1_cond_in['out_W'], 'L1_cond_out_b': _L1_cond_in['out_b'], 'L2_cond_ln1_w': _L2_cond_in['ln1_w'], 'L2_cond_ln1_b': _L2_cond_in['ln1_b'], 'L2_cond_ln2_w': _L2_cond_in['ln2_w'], 'L2_cond_ln2_b': _L2_cond_in['ln2_b'], 'L2_cond_wq': _L2_cond_in['wq'], 'L2_cond_bq': _L2_cond_in['bq'], 'L2_cond_wk': _L2_cond_in['wk'], 'L2_cond_bk': _L2_cond_in['bk'], 'L2_cond_wv': _L2_cond_in['wv'], 'L2_cond_bv': _L2_cond_in['bv'], 'L2_cond_wo': _L2_cond_in['wo'], 'L2_cond_bo': _L2_cond_in['bo'], 'L2_cond_wt_attn': _L2_cond_in['wt_attn'], 'L2_cond_bt_attn': _L2_cond_in['bt_attn'], 'L2_cond_wt_ffn': _L2_cond_in['wt_ffn'], 'L2_cond_bt_ffn': _L2_cond_in['bt_ffn'], 'L2_cond_w1': _L2_cond_in['w1'], 'L2_cond_b1': _L2_cond_in['b1'], 'L2_cond_w2': _L2_cond_in['w2'], 'L2_cond_b2': _L2_cond_in['b2'], 'L3_cond_norm_w': _L3_cond_in['norm_w'], 'L3_cond_scale_w': _L3_cond_in['scale_w'], 'L3_cond_scale_b': _L3_cond_in['scale_b'], 'L3_cond_shift_w': _L3_cond_in['shift_w'], 'L3_cond_shift_b': _L3_cond_in['shift_b'], 'L3_cond_qkv_w': _L3_cond_in['qkv_w'], 'L3_cond_proj_w': _L3_cond_in['proj_w'], 'L3_cond_proj_b': _L3_cond_in['proj_b'], 'L3_cond_mlp_w1': _L3_cond_in['mlp_w1'], 'L3_cond_mlp_b1': _L3_cond_in['mlp_b1'], 'L3_cond_mlp_w2': _L3_cond_in['mlp_w2'], 'L3_cond_mlp_b2': _L3_cond_in['mlp_b2']}

def reference(x, cond_1024, mask_BxS_ik0, L0_cond_wq, L0_cond_wk, L0_cond_wv, L0_cond_wo, L0_cond_w1, L0_cond_b1, L0_cond_w2, L0_cond_b2, L0_cond_wc, L0_cond_bc, L1_cond_norm_g, L1_cond_norm_b, L1_cond_Wq, L1_cond_bq, L1_cond_Wk, L1_cond_bk, L1_cond_Wv, L1_cond_bv, L1_cond_emb_W, L1_cond_emb_b, L1_cond_sn_g, L1_cond_sn_b, L1_cond_out_W, L1_cond_out_b, L2_cond_ln1_w, L2_cond_ln1_b, L2_cond_ln2_w, L2_cond_ln2_b, L2_cond_wq, L2_cond_bq, L2_cond_wk, L2_cond_bk, L2_cond_wv, L2_cond_bv, L2_cond_wo, L2_cond_bo, L2_cond_wt_attn, L2_cond_bt_attn, L2_cond_wt_ffn, L2_cond_bt_ffn, L2_cond_w1, L2_cond_b1, L2_cond_w2, L2_cond_b2, L3_cond_norm_w, L3_cond_scale_w, L3_cond_scale_b, L3_cond_shift_w, L3_cond_shift_b, L3_cond_qkv_w, L3_cond_proj_w, L3_cond_proj_b, L3_cond_mlp_w1, L3_cond_mlp_b1, L3_cond_mlp_w2, L3_cond_mlp_b2):
    import jax
    import jax.numpy as jnp

    def _L0_cond_ref(x, c, wq, wk, wv, wo, w1, b1, w2, b2, wc, bc):
        import jax, jax.numpy as jnp
        import numpy as np
        D = 128
        H = 16
        HKV = 4
        HD = D // H
        REP = H // HKV
        DFF = 512
        B, N = (4, 256)
        EPS = 1e-05
        WSCALE = 0.02

        def _ln(x):
            m = jnp.mean(x, axis=-1, keepdims=True)
            v = jnp.mean(jnp.square(x - m), axis=-1, keepdims=True)
            return (x - m) * jax.lax.rsqrt(v + EPS)

        def _gqa_attn(h, wq, wk, wv, wo):
            b, n, d = h.shape
            q = (h @ wq.T).reshape(b, n, HKV, REP, HD)
            k = (h @ wk.T).reshape(b, n, HKV, HD)
            v = (h @ wv.T).reshape(b, n, HKV, HD)
            scores = jnp.einsum('bqgrh,bkgh->bgrqk', q, k) * (1.0 / np.sqrt(HD))
            a = jax.nn.softmax(scores, axis=-1)
            out = jnp.einsum('bgrqk,bkgh->bqgrh', a, v).reshape(b, n, d)
            return out @ wo.T

        def _mlp(h, w1, b1, w2, b2):
            h = jax.nn.gelu(h @ w1.T + b1, approximate=False)
            return h @ w2.T + b2
        cond = jax.nn.silu(c) @ wc.T + bc
        sh1, sc1, g1, sh2, sc2, g2 = jnp.split(cond, 6, axis=-1)
        sh1, sc1, g1 = (sh1[:, None], sc1[:, None], g1[:, None])
        sh2, sc2, g2 = (sh2[:, None], sc2[:, None], g2[:, None])
        h = _ln(x) * (1.0 + sc1) + sh1
        x = x + g1 * _gqa_attn(h, wq, wk, wv, wo)
        h = _ln(x) * (1.0 + sc2) + sh2
        x = x + g2 * _mlp(h, w1, b1, w2, b2)
        return x

    def _L1_cond_ref(x, emb, gate_msa, norm_g, norm_b, Wq, bq, Wk, bk, Wv, bv, emb_W, emb_b, sn_g, sn_b, out_W, out_b):
        import jax, jax.numpy as jnp
        import numpy as np
        H = 16
        EPS = 1e-05

        def layer_norm(x, g, b):
            mu = jnp.mean(x, axis=-1, keepdims=True)
            var = jnp.var(x, axis=-1, keepdims=True)
            return (x - mu) * jax.lax.rsqrt(var + EPS) * g + b
        B, T, D = x.shape
        dh = D // H
        xn = layer_norm(x, norm_g, norm_b)
        q = (xn @ Wq + bq).reshape(B, T, H, dh)
        k = (xn @ Wk + bk).reshape(B, T, H, dh)
        v = (xn @ Wv + bv).reshape(B, T, H, dh)
        q = jax.nn.softmax(q, axis=-1)
        k = jax.nn.softmax(k, axis=1)
        ctx = jnp.einsum('bnhd,bnhl->bhdl', k, v)
        y = jnp.einsum('bnhd,bhdl->bnhl', q, ctx).reshape(B, T, D)
        emb_out = jax.nn.silu(emb) @ emb_W + emb_b
        scale, shift = jnp.split(emb_out, 2, axis=-1)
        h = layer_norm(y, sn_g, sn_b) * (1.0 + scale) + shift
        h = jax.nn.silu(h) @ out_W + out_b
        return x + gate_msa * h

    def _L2_cond_ref(x, t_emb, ln1_w, ln1_b, ln2_w, ln2_b, wq, bq, wk, bk, wv, bv, wo, bo, wt_attn, bt_attn, wt_ffn, bt_ffn, w1, b1, w2, b2):
        import math
        import jax, jax.numpy as jnp
        import numpy as np
        D_MODEL = 128
        N_HEADS = 16
        FFN_DIM = 512
        EPS = 1e-05

        def _layernorm(x, w, b):
            mu = jnp.mean(x, axis=-1, keepdims=True)
            var = jnp.var(x, axis=-1, keepdims=True)
            return (x - mu) * jax.lax.rsqrt(var + EPS) * w + b

        def _modulate(x, shift, scale):
            return x * (1.0 + scale[:, None, :]) + shift[:, None, :]
        B, S, D = x.shape
        H = N_HEADS
        hd = D // H
        residual = x
        xn = _layernorm(x, ln1_w, ln1_b)
        t_attn = t_emb @ wt_attn + bt_attn
        shift_a, scale_a = jnp.split(t_attn, 2, axis=-1)
        xn = _modulate(xn, shift_a, scale_a)
        q = (xn @ wq + bq).reshape(B, S, H, hd).transpose(0, 2, 1, 3)
        k = (xn @ wk + bk).reshape(B, S, H, hd).transpose(0, 2, 1, 3)
        v = (xn @ wv + bv).reshape(B, S, H, hd).transpose(0, 2, 1, 3)
        scores = jnp.einsum('bhqd,bhkd->bhqk', q, k) / math.sqrt(hd)
        attn = jax.nn.softmax(scores, axis=-1)
        out = jnp.einsum('bhqk,bhkd->bhqd', attn, v)
        out = out.transpose(0, 2, 1, 3).reshape(B, S, D)
        x = residual + (out @ wo + bo)
        residual = x
        xn = _layernorm(x, ln2_w, ln2_b)
        t_ffn = t_emb @ wt_ffn + bt_ffn
        shift_f, scale_f = jnp.split(t_ffn, 2, axis=-1)
        xn = _modulate(xn, shift_f, scale_f)
        h = jax.nn.gelu(xn @ w1 + b1, approximate=False)
        x = residual + (h @ w2 + b2)
        return x

    def _L3_cond_ref(x, c, attention_mask, norm_w, scale_w, scale_b, shift_w, shift_b, qkv_w, proj_w, proj_b, mlp_w1, mlp_b1, mlp_w2, mlp_b2):
        import jax, jax.numpy as jnp
        import numpy as np
        EMBED = 128
        HEADS = 16
        HEAD_DIM = EMBED // HEADS
        MLP = 4 * EMBED
        EPS = 1e-06

        def _adaln(x, c, norm_w, scale_w, scale_b, shift_w, shift_b):
            sc = jax.nn.silu(c)
            shift = sc @ shift_w.T + shift_b
            scale = jnp.clip(sc @ scale_w.T + scale_b + 1.0, 0.1, 10.0)
            norm = jnp.maximum(jnp.linalg.norm(x, axis=-1, keepdims=True) * x.shape[-1] ** (-0.5), EPS)
            h = x / norm * norm_w
            return h * scale[:, None, :] + shift[:, None, :]

        def _attention(x, attention_mask, qkv_w, proj_w, proj_b):
            B, N, C = x.shape
            qkv = (x @ qkv_w.T).reshape(B, N, 3, HEADS, HEAD_DIM)
            q = qkv[:, :, 0].transpose(0, 2, 1, 3)
            k = qkv[:, :, 1].transpose(0, 2, 1, 3)
            v = qkv[:, :, 2].transpose(0, 2, 1, 3)
            attn = jnp.einsum('bhnd,bhmd->bhnm', q, k) * HEAD_DIM ** (-0.5)
            mask = attention_mask[:, None, None, :]
            attn = jnp.where(mask == 0, -jnp.inf, attn)
            all_inf = jnp.all(attn == -jnp.inf, axis=-1, keepdims=True)
            attn = jnp.where(all_inf, 0.0, attn)
            p = jax.nn.softmax(attn, axis=-1)
            out = jnp.einsum('bhnm,bhmd->bhnd', p, v).transpose(0, 2, 1, 3).reshape(B, N, C)
            return out @ proj_w.T + proj_b

        def _mlp(x, w1, b1, w2, b2):
            h = x @ w1.T + b1
            x1, x2 = jnp.split(h, 2, axis=-1)
            return jax.nn.silu(x1) * x2 @ w2.T + b2
        x = x + _attention(_adaln(x, c, norm_w, scale_w, scale_b, shift_w, shift_b), attention_mask, qkv_w, proj_w, proj_b)
        x = x + _mlp(_adaln(x, c, norm_w, scale_w, scale_b, shift_w, shift_b), mlp_w1, mlp_b1, mlp_w2, mlp_b2)
        return x
    x = _L0_cond_ref(x, cond_1024, L0_cond_wq, L0_cond_wk, L0_cond_wv, L0_cond_wo, L0_cond_w1, L0_cond_b1, L0_cond_w2, L0_cond_b2, L0_cond_wc, L0_cond_bc)
    x = _L1_cond_ref(x, cond_1024[:, None, :], cond_1024[:, None, :], L1_cond_norm_g, L1_cond_norm_b, L1_cond_Wq, L1_cond_bq, L1_cond_Wk, L1_cond_bk, L1_cond_Wv, L1_cond_bv, L1_cond_emb_W, L1_cond_emb_b, L1_cond_sn_g, L1_cond_sn_b, L1_cond_out_W, L1_cond_out_b)
    x = _L2_cond_ref(x, cond_1024, L2_cond_ln1_w, L2_cond_ln1_b, L2_cond_ln2_w, L2_cond_ln2_b, L2_cond_wq, L2_cond_bq, L2_cond_wk, L2_cond_bk, L2_cond_wv, L2_cond_bv, L2_cond_wo, L2_cond_bo, L2_cond_wt_attn, L2_cond_bt_attn, L2_cond_wt_ffn, L2_cond_bt_ffn, L2_cond_w1, L2_cond_b1, L2_cond_w2, L2_cond_b2)
    x = _L3_cond_ref(x, cond_1024, mask_BxS_ik0, L3_cond_norm_w, L3_cond_scale_w, L3_cond_scale_b, L3_cond_shift_w, L3_cond_shift_b, L3_cond_qkv_w, L3_cond_proj_w, L3_cond_proj_b, L3_cond_mlp_w1, L3_cond_mlp_b1, L3_cond_mlp_w2, L3_cond_mlp_b2)
    return x

_drawn_inputs = setup_inputs


def setup_inputs(seed=0):
    import zlib

    import numpy as np

    out = dict(_drawn_inputs(seed))
    spreads = {'L0_cond_b1': (0.0, 0.8),
     'L0_cond_b2': (0.0, 0.484),
     'L0_cond_bc': (0.0, 0.794),
     'L1_cond_norm_g': (1.0, 0.6),
     'L1_cond_norm_b': (0.0, 0.8),
     'L1_cond_bq': (0.0, 2.0),
     'L1_cond_bk': (0.0, 2.0),
     'L1_cond_bv': (0.0, 0.375),
     'L1_cond_emb_b': (0.0, 1.283),
     'L1_cond_sn_g': (1.0, 0.6),
     'L1_cond_sn_b': (0.0, 2.0),
     'L1_cond_out_b': (0.0, 0.424),
     'L2_cond_ln1_w': (1.0, 0.6),
     'L2_cond_ln1_b': (0.0, 0.8),
     'L2_cond_ln2_w': (1.0, 0.6),
     'L2_cond_ln2_b': (0.0, 2.0),
     'L2_cond_bq': (0.0, 2.0),
     'L2_cond_bk': (0.0, 2.0),
     'L2_cond_bv': (0.0, 1.759),
     'L2_cond_bo': (0.0, 0.381),
     'L2_cond_bt_attn': (0.0, 0.8),
     'L2_cond_bt_ffn': (0.0, 2.0),
     'L2_cond_b1': (0.0, 1.27),
     'L2_cond_b2': (0.0, 0.432),
     'L3_cond_norm_w': (1.0, 0.6)}
    factors = {'L0_cond_wq': 8.0,
     'L0_cond_wk': 8.0,
     'L0_cond_wv': 8.0,
     'L0_cond_wo': 8.0,
     'L0_cond_w1': 6.308,
     'L0_cond_w2': 5.758,
     'L0_cond_wc': 3.43,
     'L1_cond_Wq': 51.667,
     'L1_cond_Wk': 43.037,
     'L2_cond_wq': 8.0,
     'L2_cond_wk': 8.0,
     'L2_cond_wv': 3.552,
     'L2_cond_wt_attn': 4.779,
     'L2_cond_wt_ffn': 10.059,
     'L3_cond_scale_w': 8.0,
     'L3_cond_scale_b': 8.0,
     'L3_cond_shift_w': 7.775,
     'L3_cond_shift_b': 8.0,
     'L3_cond_mlp_w1': 4.392,
     'L3_cond_mlp_b1': 8.0,
     'L3_cond_mlp_w2': 4.404,
     'L3_cond_mlp_b2': 22.616,
     'L1_cond_emb_W': 7.878,
     'L3_cond_qkv_w': 3.094,
     'L3_cond_proj_w': 2.844,
     'L3_cond_proj_b': 8.0}
    for name, (base, spread) in spreads.items():
        noise = np.random.default_rng([zlib.crc32(name.encode()), seed]).standard_normal(out[name].shape)
        drawn = base * np.exp(spread * noise) if base else spread * noise
        out[name] = jnp.asarray(drawn.astype(out[name].dtype))
    for name, factor in factors.items():
        out[name] = (out[name] * factor).astype(out[name].dtype)
    return out
```

```python
from contextlib import ExitStack

import concourse.bass as bass
from concourse import mybir

F32 = mybir.dt.float32
BF16 = mybir.dt.bfloat16
I32 = mybir.dt.int32
ALU = mybir.AluOpType
ACT = mybir.ActivationFunctionType
AX = mybir.AxisListType

B, T, D = 8, 128, 128
H, HD = 16, 8
GH = 4
NG = H // GH
U = 4
S = B // U
N = S * T
F = 512
FC = F // D
NATT = 3
NGROUPS = NATT * B * NG
NSEQ = NATT * B
MASKED = -1e30

WEIGHTS = [
    ("cond0", 6 * D), ("q0", D), ("k0", D), ("v0", D), ("o0", D), ("up0", F), ("down0", F),
    ("cond1", 2 * D), ("q1", D), ("k1", D), ("v1", D), ("o1", D),
    ("cond2a", 2 * D), ("cond2m", 2 * D), ("q2", D), ("k2", D), ("v2", D), ("o2", D), ("up2", F), ("down2", F),
    ("cond3", 2 * D), ("q3", D), ("k3", D), ("v3", D), ("o3", D), ("up3", 2 * F), ("down3", F),
]
LOADS = [("cond0",), ("q0", "k0", "v0"), ("o0", "up0", "down0"), ("cond1", "q1", "k1", "v1", "o1"),
         ("cond2a", "cond2m", "q2", "k2", "v2", "o2"), ("up2", "down2"), ("cond3", "q3", "k3", "v3", "o3"),
         ("up3", "down3")]
VECTORS = [
    ("c", B), ("bc0", 6), ("bup0", FC), ("bdown0", 1),
    ("g1", 1), ("b1", 1), ("bk1", 1), ("bcond1", 2), ("gs1", 1), ("bs1", 1), ("bo1", 1),
    ("g2a", 1), ("b2a", 1), ("g2m", 1), ("b2m", 1), ("bq2", 1), ("bk2", 1), ("bv2", 1), ("bo2", 1),
    ("bcond2a", 2), ("bcond2m", 2), ("bup2", FC), ("bdown2", 1),
    ("g3", 1), ("bcond3", 2), ("bo3", 1), ("bup3", 2 * FC), ("bdown3", 1),
]
CONST = 2 * D + GH + NG + S
NORMS = ["0a", "0m", "1a", "1s", "2a", "2m", "3a", "3m"]
EPS = 1e-5
EPS3 = 1e-6


def columns(items):
    at, out = 0, {}
    for name, n in items:
        out[name] = slice(at, at + n)
        at += n
    return out, at


WCOL, WTOTAL = columns(WEIGHTS)
VCOL, VTOTAL = columns(VECTORS)


def norm_steps(which, bank0, bank1):
    return [("stats", which, (bank0,)), ("normed", which, ()), ("turned", which, (bank1,))]


def plan():
    out = []

    def spread(u, first, step, steps):
        out.extend((first + i * step, u, *s) for i, s in enumerate(steps))

    for u in range(U):
        m = (u % 3,)
        first, step = [(-12, 1), (-11, 1), (-2, 1.5), (5, 1.5)][u]
        spread(u, first, step, [("enter", 0, m), ("stats", "0a", ()), ("normed", "0a", ()), ("turned", "0a", m),
                                ("qk", 0, m), ("v", 0, m)])
        end = S * NG * (u + 1)
        spread(u, end + 4, 0.8, [
            ("out", 0, (0,)), *norm_steps("0m", 1, 0), ("up", 0, (0, 1)), ("down", 0, (0,)),
            *norm_steps("1a", 1, 1), ("lin_qk", 1, (2,)), ("lin_v", 1, (2,)), ("lin_turn", 1, (2,)),
            ("lin_ctx", 1, (2,)), ("lin_y", 1, (2,)), ("normed", "1s", ()), ("turned", "1s", (2,)),
            ("lin_out", 1, (2,)), *norm_steps("2a", 2, 2), ("qk", 2, (2,)), ("v", 2, (2,))])
        end += B * NG
        spread(u, end + 4, 1.6, [
            ("out", 2, (0,)), *norm_steps("2m", 1, 0), ("up", 2, (0, 1)), ("down", 2, (0,)),
            *norm_steps("3a", 2, 2), ("qk", 3, (2,)), ("v", 3, (2,))])
        end += B * NG
        spread(u, end + 4, 1.6, [
            ("out", 3, (0,)), *norm_steps("3m", 2 if u else 1, 2), *[("gated", c, (c % 2,)) for c in range(FC)],
            ("down", 3, (2,)), ("leave", 3, (2,))])
    out.append((-20, 0, "cond", "0", (2,)))
    for name, slot in (("1", 1.1), ("2a", 2.1), ("2m", 3.1), ("3", 4.1)):
        out.append((slot, 0, "cond", name, (2,)))
    out.sort(key=lambda x: x[0])
    for i, (_, u, kind, which, banks) in enumerate(out):
        if kind == "stats" and banks:
            upto = next(k for k, s in enumerate(out) if s[1:4] == (u, "normed", which))
            assert not any(set(s[4]) & set(banks) for s in out[i + 1:upto]), (u, which)
    return out


def build(nc, x_in, c_in, w_in, rows_in, mask_in, const_in, out):
    with ExitStack() as ctx:
        def sb(name, shape, dt=F32):
            return ctx.enter_context(nc.sbuf_tensor(name, shape, dt))

        def sem(name):
            return ctx.enter_context(nc.semaphore(name))

        def sems(name, n):
            return [sem(f"{name}{i}") for i in range(n)]

        w = sb("w", [128, WTOTAL])
        vec = sb("vec", [128, VTOTAL])
        rows = sb("rows", [128, 2, 1, D])
        mask_i = sb("mask_i", [128, B, T], I32)
        masked = sb("masked", [128, B, 1, T], BF16)
        first_row = sb("first_row", [128, T], BF16)
        const = sb("const", [128, CONST])
        ident = const[:, 0:D]
        blocks = const[:, D:2 * D]
        of_head = const[:, 2 * D:2 * D + GH]
        of_strip = const[:, 2 * D + GH:2 * D + GH + NG]
        minus_half = const[:, 2 * D + GH + NG:CONST]

        x_tok = sb("x_tok", [128, B, D])
        y_tok = sb("y_tok", [128, B, D])

        def per_unit(name, shape, n=U):
            tiles = [sb(f"{name}{i}", shape) for i in range(n)]
            return [tiles[u % n] for u in range(U)]

        xT = per_unit("xT", [128, S, T])
        xhat = per_unit("xhat", [128, S, D])
        hT = per_unit("hT", [128, S, T])
        qT = per_unit("qT", [128, S, T])
        kT = per_unit("kT", [128, S, T])
        q_strip = per_unit("q_strip", [128, S, NG, T])
        k_head = per_unit("k_head", [128, S, GH, T])
        v_pad = per_unit("v_pad", [128, S, H, 32])
        att = per_unit("att", [128, S, T])
        scaled = per_unit("scaled", [128, S, T], 2)
        hid = per_unit("hid", [128, FC, N], 2)
        th = sb("th", [128, 2, N])
        half = sb("half", [128, 2, N])
        silu_g = sb("silu_g", [128, 2, N])
        bn = sb("bn", [128, U, S, 6])
        mv = sb("mv", [128, U, S, 2])
        base = sb("base", [128, U, S])
        rstd = sb("rstd", [128, U, S])
        l_q = per_unit("l_q", [128, S, D], 2)
        l_qs = per_unit("l_qs", [128, S, D], 2)
        l_k = per_unit("l_k", [128, S, T], 2)
        l_v = per_unit("l_v", [128, S, D], 2)
        l_e = per_unit("l_e", [128, 2, S, T], 2)
        l_eT = per_unit("l_eT", [128, 2 * S * T], 2)
        l_ctx = per_unit("l_ctx", [128, S, D], 2)
        l_y = per_unit("l_y", [128, S, D], 2)
        l_t = per_unit("l_t", [128, S, T], 2)
        l_hs = per_unit("l_hs", [128, S, T], 2)
        q_max = sb("q_max", [128, U, S * H])
        q_sum = sb("q_sum", [128, U, S * H])
        q_inv = sb("q_inv", [128, U, S * H])
        k_max = sb("k_max", [128, U, S])
        k_sum = sb("k_sum", [128, U, S])
        k_inv = sb("k_inv", [128, U, S])
        c_tanh = sb("c_tanh", [128, B])
        c_half = sb("c_half", [128, B])
        sil = sb("sil", [128, B])
        cnd = sb("cnd", [128, 14, B])
        tmp = sb("tmp", [128, 2, B])
        mod_a = sb("mod_a", [128, len(NORMS), B])
        mod_b = sb("mod_b", [128, len(NORMS), B])
        bq2_scaled = sb("bq2_scaled", [128, 1])
        bo2_full = sb("bo2_full", [128, 1])
        bup3_half = sb("bup3_half", [128, FC])
        probs = sb("probs", [128, 4, GH, T])
        probsT = sb("probsT", [128, 2, H, T])
        neg_max = sb("neg_max", [128, NGROUPS, GH])
        den = sb("den", [128, NSEQ, H])
        rden = sb("rden", [128, NSEQ, H, 1])
        rden_wide = sb("rden_wide", [128, 2, H, HD])
        rdenT = sb("rdenT", [128, 2, T])

        psum = [ctx.enter_context(nc.psum_tensor(f"ps{i}", [128, 512], F32)) for i in range(8)]
        ps_scores, ps_turned, ps_att, ps_dense = psum[0:2], psum[2:4], psum[4], psum[5:8]

        x_loaded, vec_loaded, const_loaded, row_loaded = sem("x_loaded"), sem("vec_loaded"), sem("const_loaded"), sem("row_loaded")
        w_loaded = sems("w_loaded", len(LOADS))
        stored = sem("stored")
        c_tanh_ready, silu_ready = sem("c_tanh_ready"), sem("silu_ready")
        cond_ready = sem("cond_ready")
        filled = sems("filled", 3)
        drained = sems("drained", 3)
        x_ready = sems("x_ready", U)
        var_ready, rstd_ready, xhat_ready = sems("var_ready", U), sems("rstd_ready", U), sems("xhat_ready", U)
        qk_ready = sems("qk_ready", U)
        lin_sub, lin_exp = sems("lin_sub", U), sems("lin_exp", U)
        lin_tanh, lin_silu = sems("lin_tanh", U), sems("lin_silu", U)
        gate_halves = sem("gate_halves")
        y_ready = sem("y_ready")
        scores_ready, max_ready, probs_ready = sem("scores_ready"), sem("max_ready"), sem("probs_ready")
        turned_ready, turned_read = sem("turned_ready"), sem("turned_read")
        rden_ready, att_ready, rdenT_ready, att_read = sem("rden_ready"), sem("att_ready"), sem("rdenT_ready"), sem("att_read")
        dve_own = sem("dve_own")

        STEPS = plan()
        FIRST, LAST = int(STEPS[0][0]) - 1, int(STEPS[-1][0]) + 2
        step_of = {(s[1], s[2], s[3]): s for s in STEPS}
        before, fills, drains, last_of = {}, {}, {}, {}
        n_fill, n_drain = [0, 0, 0], [0, 0, 0]
        SUMS = [("enter", 0), ("out", 0), ("down", 0), ("lin_out", 1), ("out", 2), ("down", 2), ("out", 3), ("down", 3)]
        BEFORE_NORM = {"0m": 2, "1a": 3, "2a": 4, "2m": 5, "3a": 6, "3m": 7}
        for s in STEPS:
            for b in s[4]:
                before[s, b] = last_of.get(b)
                last_of[b] = s
                n_fill[b] += 1
                fills[s, b] = n_fill[b]
                if (s[2], s[3]) not in SUMS and s[2] != "leave":
                    n_drain[b] += 1
                    drains[s, b] = n_drain[b]
        gated_no = {s: i for i, s in enumerate(x for x in STEPS if x[2] == "gated")}

        def slots():
            for t in range(FIRST, LAST):
                yield t, [s for s in STEPS if int(s[0] - FIRST) + FIRST == t]

        def wait_done(eng, step, b):
            _, u, kind, arg, _ = step
            if (kind, arg) in SUMS:
                eng.wait_ge(x_ready[u], SUMS.index((kind, arg)) + 1)
            elif kind == "leave":
                eng.wait_ge(y_ready, u + 1)
            else:
                eng.wait_ge(drained[b], drains[step, b])

        def wait_written(eng, u, kind, arg):
            step = step_of[u, kind, arg]
            for b in step[4]:
                wait_done(eng, step, b)

        def wait_free(eng, step, b):
            if before[step, b] is not None:
                wait_done(eng, before[step, b], b)

        def wait_filled(eng, step, b):
            eng.wait_ge(filled[b], fills[step, b])

        def wait_weights(eng, name):
            eng.wait_ge(w_loaded[next(i for i, names in enumerate(LOADS) if name in names)], 16)

        def vcol(name, i=0):
            at = VCOL[name].start + i
            return vec[:, at:at + 1]

        def wcol(name, i=0):
            at = WCOL[name].start + i * D
            return w[:, at:at + D]

        def att_no(layer):
            return (0, 2, 3).index(layer)

        def group(g):
            a, r = divmod(g, B * NG)
            u, r = divmod(r, S * NG)
            return (0, 2, 3)[a], u, r // NG, r % NG

        def by_seq(tile):
            return tile.rearrange("p (s t) -> p s t", s=S)

        NO = {n: i for i, n in enumerate(NORMS)}
        block = ctx.enter_context(nc.Block())

        @block.sync
        def _(sp):
            sp.dma_start(vec[:, :], c_in).then_inc(vec_loaded, 16)
            sp.dma_start(x_tok[:, :, :], x_in.rearrange("b t d -> t b d")).then_inc(x_loaded, 16)
            for i in range(1, len(LOADS), 2):
                cols = slice(WCOL[LOADS[i][0]].start, WCOL[LOADS[i][-1]].stop)
                sp.dma_start(w[:, cols], w_in[:, cols]).then_inc(w_loaded[i], 16)
            for u in range(U):
                sp.wait_ge(y_ready, u + 1)
                sp.dma_start(out.rearrange("b t d -> t b d")[:, u * S:(u + 1) * S, :],
                             y_tok[:, u * S:(u + 1) * S, :]).then_inc(stored, 16)
            sp.wait_ge(stored, 16 * U)

        @block.gpsimd
        def _(pool):
            pool.dma_start(rows[:, :, :, :].rearrange("p a o d -> p (a o d)"), rows_in.partition_broadcast(128)).then_inc(row_loaded, 16)
            pool.dma_start(mask_i[:, :, :].rearrange("p b t -> p (b t)"), mask_in.partition_broadcast(128)).then_inc(row_loaded, 16)

            def power(u, which):
                pool.wait_ge(var_ready[u], NO[which] + 1)
                nc.gpsimd.tensor_tensor(rstd[:, u, :], base[:, u, :], minus_half, ALU.pow).then_inc(rstd_ready[u], 1)

            def operands(step):
                _, u, _, layer, (b,) = step
                wait_done(pool, step, b)
                for j in range(NG):
                    nc.gpsimd.tensor_scalar(q_strip[u][:, :, j, :], qT[u][:, :, :], of_strip[:, j:j + 1], 0.0,
                                            ALU.mult, ALU.add)
                for i in range(GH):
                    last = nc.gpsimd.tensor_scalar(k_head[u][:, :, i, :], kT[u][:, :, :], of_head[:, i:i + 1], 0.0,
                                                   ALU.mult, ALU.add)
                last.then_inc(qk_ready[u], 1)

            pool.wait_ge(const_loaded, 16)
            for t, steps in slots():
                for step in steps:
                    if step[2] == "stats":
                        power(step[1], step[3])
                    if step[2] == "lin_y":
                        power(step[1], "1s")
                    if step[2] == "qk":
                        operands(step)

        @block.scalar
        def _(act):
            cols = slice(WCOL[LOADS[0][0]].start, WCOL[LOADS[0][-1]].stop)
            act.dma_start(w[:, cols], w_in[:, cols]).then_inc(w_loaded[0], 16)
            act.dma_start(const[:, :], const_in).then_inc(const_loaded, 16)
            for i in range(2, len(LOADS), 2):
                cols = slice(WCOL[LOADS[i][0]].start, WCOL[LOADS[i][-1]].stop)
                act.dma_start(w[:, cols], w_in[:, cols]).then_inc(w_loaded[i], 16)
            act.wait_ge(vec_loaded, 16)
            nc.scalar.activation(c_tanh[:, :], vec[:, VCOL["c"]], ACT.Tanh, scale=0.5).then_inc(c_tanh_ready, 1)

            def exps(g):
                act.wait_ge(max_ready, g + 1)
                if g >= 4:
                    act.wait_ge(turned_ready, g - 3)
                for i in range(GH):
                    last = nc.scalar.activation(probs[:, g % 4, i, :], ps_scores[g % 2][:, i * T:(i + 1) * T], ACT.Exp,
                                                bias=neg_max[:, g, i:i + 1],
                                                accum_out=den[:, g // NG, GH * (g % NG) + i:GH * (g % NG) + i + 1])
                last.then_inc(probs_ready, 1)

            def inverse_sums(q):
                act.wait_ge(att_ready, q + 1)
                nc.scalar.activation(rdenT[:, q % 2, :], ps_att[:, T:2 * T], ACT.Copy).then_inc(rdenT_ready, 1)

            def dense(step):
                _, u, kind, arg, banks = step
                ps = [ps_dense[b] for b in banks]
                if kind == "enter":
                    wait_filled(act, step, banks[0])
                    nc.scalar.activation(xT[u][:, :, :], by_seq(ps[0][:, 0:N]), ACT.Copy).then_inc(x_ready[u], 1)
                if kind == "turned":
                    wait_filled(act, step, banks[0])
                    act.wait_ge(cond_ready, {"0": 1, "1": 2, "2": 4, "3": 5}[arg[0]])
                    for s in range(S):
                        i = S * u + s
                        last = nc.scalar.activation(hT[u][:, s, :], ps[0][:, s * T:(s + 1) * T], ACT.Identity,
                                                    scale=mod_a[:, NO[arg], i:i + 1], bias=mod_b[:, NO[arg], i:i + 1])
                    last.then_inc(drained[banks[0]], 1)
                    if arg == "1s":
                        wait_done(act, step, banks[0])
                        nc.scalar.activation(l_t[u][:, :, :], hT[u][:, :, :], ACT.Tanh).then_inc(lin_tanh[u], 1)
                if kind == "qk":
                    wait_filled(act, step, banks[0])
                    q, k = by_seq(ps[0][:, 0:N]), by_seq(ps[0][:, N:2 * N])
                    if arg == 2:
                        nc.scalar.activation(qT[u][:, :, :], q, ACT.Identity, scale=HD ** -0.5, bias=bq2_scaled[:, :])
                        last = nc.scalar.activation(kT[u][:, :, :], k, ACT.Identity, bias=vcol("bk2"))
                    else:
                        nc.scalar.activation(qT[u][:, :, :], q, ACT.Copy, scale=HD ** -0.5)
                        last = nc.scalar.activation(kT[u][:, :, :], k, ACT.Copy)
                    last.then_inc(drained[banks[0]], 1)
                if kind == "up":
                    for h in range(2):
                        wait_filled(act, step, banks[h])
                        for c in (2 * h, 2 * h + 1):
                            last = nc.scalar.activation(hid[u][:, c, :], ps[h][:, (c % 2) * N:(c % 2 + 1) * N], ACT.Gelu,
                                                        bias=vcol(f"bup{arg}", c))
                        last.then_inc(drained[banks[h]], 1)
                if kind == "gated":
                    n = gated_no[step]
                    wait_filled(act, step, banks[0])
                    if n >= 2:
                        prev = list(gated_no)[n - 2]
                        wait_done(act, prev, prev[4][0])
                    nc.scalar.activation(th[:, n % 2, :], ps[0][:, 0:N], ACT.Tanh, scale=0.5, bias=bup3_half[:, arg:arg + 1])
                    nc.scalar.activation(half[:, n % 2, :], ps[0][:, 0:N], ACT.Identity, scale=0.5,
                                         bias=bup3_half[:, arg:arg + 1]).then_inc(gate_halves, 1)
                if kind == "lin_qk":
                    act.wait_ge(lin_sub[u], 1)
                    nc.scalar.activation(l_e[u][:, 0, :, :], l_qs[u][:, :, :], ACT.Exp)
                    for s in range(S):
                        last = nc.scalar.activation(l_e[u][:, 1, s, :], l_k[u][:, s, :], ACT.Exp, bias=k_max[:, u, s:s + 1],
                                                    accum_out=k_sum[:, u, s:s + 1])
                    last.then_inc(lin_exp[u], 1)
                if kind == "lin_turn":
                    wait_filled(act, step, banks[0])
                    nc.scalar.activation(l_eT[u][:, :], ps[0][:, :], ACT.Copy).then_inc(drained[banks[0]], 1)
                if kind == "leave":
                    wait_filled(act, step, banks[0])
                    nc.scalar.activation(y_tok[:, u * S:(u + 1) * S, :], by_seq(ps[0][:, 0:N]), ACT.Copy).then_inc(y_ready, 1)

            for t, steps in slots():
                if 0 <= t < NGROUPS:
                    exps(t)
                if t >= 7 and (t - 7) % NG == 0 and (t - 7) // NG < NSEQ:
                    inverse_sums((t - 7) // NG)
                for step in steps:
                    dense(step)

        @block.vector
        def _(dve):
            own = [0]

            def link(ins):
                own[0] += 1
                ins.then_inc(dve_own, 1)
                dve.wait_ge(dve_own, own[0])

            for u in range(U):
                nc.vector.memset(v_pad[u][:, :, :, :], 0.0)
            link(nc.vector.memset(first_row[:, :], 0.0))
            nc.vector.memset(first_row[0:1, :], 1.0)
            dve.wait_ge(vec_loaded, 16)
            nc.vector.tensor_scalar(bq2_scaled[:, :], vcol("bq2"), HD ** -0.5, None, ALU.mult)
            nc.vector.tensor_scalar(bup3_half[:, :], vec[:, VCOL["bup3"].start:VCOL["bup3"].start + FC], 0.5, None, ALU.mult)
            link(nc.vector.tensor_scalar(c_half[:, :], vec[:, VCOL["c"]], 0.5, None, ALU.mult))
            dve.wait_ge(c_tanh_ready, 1)
            nc.vector.scalar_tensor_tensor(sil[:, :], c_tanh[:, :], 1.0, c_half[:, :], ALU.add, ALU.mult).then_inc(silu_ready, 1)

            def maxima(g):
                dve.wait_ge(scores_ready, g + 1)
                nc.vector.tensor_reduce(neg_max[:, g, :], ps_scores[g % 2][:, :].rearrange("p (h k) -> p h k", h=GH), AX.X,
                                        ALU.max, negate=True).then_inc(max_ready, 1)

            def turned_out(g):
                dve.wait_ge(turned_ready, g + 1)
                q = g // NG
                if q >= 2 and g % NG == 0:
                    dve.wait_ge(att_ready, q - 1)
                nc.vector.tensor_copy(probsT[:, q % 2, GH * (g % NG):GH * (g % NG + 1), :].rearrange("p h t -> p (h t)"),
                                      ps_turned[g % 2][:, :]).then_inc(turned_read, 1)

            def inverse(q):
                dve.wait_ge(probs_ready, NG * (q + 1))
                link(nc.vector.reciprocal(rden[:, q, :, 0], den[:, q, :]))
                if q >= 2:
                    dve.wait_ge(att_ready, q - 1)
                nc.vector.tensor_copy(rden_wide[:, q % 2, :, :], rden[:, q, :, :].broadcast_to([128, H, HD])).then_inc(rden_ready, 1)

            def normalise(q):
                _, u, s, _ = group(q * NG)
                dve.wait_ge(rdenT_ready, q + 1)
                nc.vector.tensor_tensor(att[u][:, s, :], ps_att[:, 0:T], rdenT[:, q % 2, :], ALU.mult).then_inc(att_read, 1)

            def statistics(u, which, src):
                for s in range(S):
                    last = nc.vector.bn_stats(bn[:, u, s, :], src(s))
                link(last)
                for s in range(S):
                    last = nc.vector.bn_aggr(mv[:, u, s, :], bn[:, u, s, :])
                link(last)
                if which[0] == "3":
                    link(nc.vector.tensor_tensor(base[:, u, :], mv[:, u, :, 0], mv[:, u, :, 0], ALU.mult))
                    link(nc.vector.tensor_tensor(base[:, u, :], base[:, u, :], mv[:, u, :, 1], ALU.add))
                    nc.vector.tensor_scalar(base[:, u, :], base[:, u, :], EPS3 * EPS3, None, ALU.max).then_inc(var_ready[u], 1)
                else:
                    nc.vector.tensor_scalar(base[:, u, :], mv[:, u, :, 1], EPS, None, ALU.add).then_inc(var_ready[u], 1)

            def row_source(u, which):
                if which == "0a":
                    return lambda s: x_tok[:, S * u + s, :]
                if which == "1s":
                    return lambda s: l_y[u][:, s, :]
                (b,) = step_of[u, "stats", which][4]
                return lambda s: ps_dense[b][:, s * T:(s + 1) * T]

            def add_scaled(step, name, gate):
                _, u, _, _, (b,) = step
                for s in range(S):
                    last = nc.vector.tensor_scalar(scaled[u][:, s, :], ps_dense[b][:, s * T:(s + 1) * T], vcol(name),
                                                   gate(S * u + s), ALU.add, ALU.mult)
                link(last)
                nc.vector.tensor_tensor(xT[u][:, :, :], xT[u][:, :, :], scaled[u][:, :, :], ALU.add).then_inc(x_ready[u], 1)

            def condition(step):
                _, _, _, arg, (b,) = step
                wait_filled(dve, step, b)
                ps = ps_dense[b]

                def plus_bias(first, n, name):
                    nc.vector.tensor_tensor(cnd[:, first:first + n, :], ps[:, 0:n * B].rearrange("p (i b) -> p i b", i=n),
                                            vec[:, VCOL[name]].rearrange("p (i o) -> p i o", o=1).broadcast_to([128, n, B]),
                                            ALU.add).then_inc(drained[b], 1)
                    wait_done(dve, step, b)

                def modulate(which, scale, shift, g, bias):
                    nc.vector.tensor_scalar(mod_a[:, NO[which], :], cnd[:, scale, :], 1.0, vcol(g), ALU.add, ALU.mult)
                    link(nc.vector.tensor_scalar(tmp[:, 0, :], cnd[:, scale, :], 1.0, vcol(bias), ALU.add, ALU.mult))
                    return nc.vector.tensor_tensor(mod_b[:, NO[which], :], tmp[:, 0, :], cnd[:, shift, :], ALU.add)

                if arg == "0":
                    plus_bias(0, 6, "bc0")
                    for which, i in (("0a", 0), ("0m", 3)):
                        nc.vector.tensor_scalar(mod_a[:, NO[which], :], cnd[:, i + 1, :], 1.0, None, ALU.add)
                        last = nc.vector.tensor_copy(mod_b[:, NO[which], :], cnd[:, i, :])
                    last.then_inc(cond_ready, 1)
                if arg == "1":
                    plus_bias(6, 2, "bcond1")
                    nc.vector.tensor_copy(mod_a[:, NO["1a"], :], vcol("g1").broadcast_to([128, B]))
                    nc.vector.tensor_copy(mod_b[:, NO["1a"], :], vcol("b1").broadcast_to([128, B]))
                    link(modulate("1s", 6, 7, "gs1", "bs1"))
                    for m in (mod_a, mod_b):
                        last = nc.vector.tensor_scalar(m[:, NO["1s"], :], m[:, NO["1s"], :], 0.5, None, ALU.mult)
                    last.then_inc(cond_ready, 1)
                if arg == "2a":
                    nc.vector.tensor_tensor(bo2_full[:, :], ps[:, 2 * B:2 * B + 1], vcol("bo2"), ALU.add)
                    plus_bias(8, 2, "bcond2a")
                    modulate("2a", 9, 8, "g2a", "b2a").then_inc(cond_ready, 1)
                if arg == "2m":
                    plus_bias(10, 2, "bcond2m")
                    modulate("2m", 11, 10, "g2m", "b2m").then_inc(cond_ready, 1)
                if arg == "3":
                    plus_bias(12, 2, "bcond3")
                    link(nc.vector.tensor_scalar(tmp[:, 1, :], cnd[:, 12, :], 1.0, 0.1, ALU.add, ALU.max))
                    for which in ("3a", "3m"):
                        nc.vector.tensor_scalar(mod_a[:, NO[which], :], tmp[:, 1, :], 10.0, vcol("g3"), ALU.min, ALU.mult)
                        last = nc.vector.tensor_copy(mod_b[:, NO[which], :], cnd[:, 13, :])
                    link(last)
                    dve.wait_ge(row_loaded, 32)
                    nc.vector.tensor_scalar(masked[:, :, 0, :], mask_i[:, :, :], 0.0, MASKED, ALU.is_equal, ALU.mult)\
                        .then_inc(cond_ready, 1)

            def dense(step):
                _, u, kind, arg, banks = step
                b = banks[0] if banks else None
                ps = ps_dense[b] if banks else None
                if kind == "cond":
                    condition(step)
                if kind == "stats":
                    if arg == "0a":
                        dve.wait_ge(x_loaded, 16)
                    else:
                        wait_filled(dve, step, b)
                    statistics(u, arg, row_source(u, arg))
                if kind == "normed":
                    src = row_source(u, arg)
                    dve.wait_ge(rstd_ready[u], NO[arg] + 1)
                    for s in range(S):
                        if arg[0] == "3":
                            last = nc.vector.tensor_scalar(xhat[u][:, s, :], src(s), rstd[:, u, s:s + 1], None, ALU.mult)
                        else:
                            last = nc.vector.tensor_scalar(xhat[u][:, s, :], src(s), mv[:, u, s, 0:1], rstd[:, u, s:s + 1],
                                                           ALU.subtract, ALU.mult)
                    if arg in ("0a", "1s"):
                        last.then_inc(xhat_ready[u], 1)
                    else:
                        last.then_inc(drained[step_of[u, "stats", arg][4][0]], 1)
                if kind == "v":
                    wait_filled(dve, step, b)
                    for s in range(S):
                        dst = v_pad[u][:, s, :, :].rearrange("p (j i) c -> p j (i c)", i=GH)
                        dst = bass.AP(dst.tensor, dst.offset, [dst.ap[0], [GH * 32, NG], [32 + HD, GH], [1, HD]])
                        last = nc.vector.tensor_copy(dst, ps[:, s * D:(s + 1) * D].rearrange("p (j i d) -> p j i d", j=NG, i=GH))
                    last.then_inc(drained[b], 1)
                if kind == "out" and arg == 0:
                    wait_filled(dve, step, b)
                    for s in range(S):
                        last = nc.vector.scalar_tensor_tensor(xT[u][:, s, :], ps[:, s * T:(s + 1) * T], cnd[:, 2, S * u + s:S * u + s + 1],
                                                              xT[u][:, s, :], ALU.mult, ALU.add)
                    last.then_inc(x_ready[u], 1)
                if (kind == "out" and arg) or (kind == "down" and arg):
                    wait_filled(dve, step, b)
                    bias = {("out", 2): bo2_full[:, :], ("out", 3): vcol("bo3"), ("down", 2): vcol("bdown2"),
                            ("down", 3): vcol("bdown3")}[kind, arg]
                    nc.vector.scalar_tensor_tensor(xT[u][:, :, :], by_seq(ps[:, 0:N]), bias, xT[u][:, :, :], ALU.add, ALU.add)\
                        .then_inc(x_ready[u], 1)
                if kind == "down" and arg == 0:
                    wait_filled(dve, step, b)
                    add_scaled(step, "bdown0", lambda i: cnd[:, 5, i:i + 1])
                if kind == "lin_out":
                    wait_filled(dve, step, b)
                    add_scaled(step, "bo1", lambda i: vec[:, VCOL["c"].start + i:VCOL["c"].start + i + 1])
                if kind == "gated":
                    n = gated_no[step]
                    dve.wait_ge(gate_halves, n + 1)
                    link(nc.vector.scalar_tensor_tensor(silu_g[:, n % 2, :], th[:, n % 2, :], 1.0, half[:, n % 2, :], ALU.add, ALU.mult))
                    nc.vector.scalar_tensor_tensor(hid[u][:, arg, :], ps[:, N:2 * N], vcol("bup3", FC + arg), silu_g[:, n % 2, :],
                                                   ALU.add, ALU.mult).then_inc(drained[b], 1)
                if kind == "lin_qk":
                    wait_filled(dve, step, b)
                    dve.wait_ge(row_loaded, 32)
                    nc.vector.tensor_tensor(l_q[u][:, :, :], by_seq(ps[:, 0:N]), rows[:, 0, :, :].broadcast_to([128, S, D]), ALU.add)
                    nc.vector.tensor_scalar(l_k[u][:, :, :], by_seq(ps[:, N:2 * N]), vcol("bk1"), None, ALU.add).then_inc(drained[b], 1)
                    wait_done(dve, step, b)
                    heads = l_q[u][:, :, :].rearrange("p s (h d) -> p (s h) d", d=HD)
                    nc.vector.tensor_reduce(k_max[:, u, :], l_k[u][:, :, :], AX.X, ALU.max, negate=True)
                    link(nc.vector.tensor_reduce(q_max[:, u, :], heads, AX.X, ALU.max, negate=True))
                    nc.vector.tensor_tensor(l_qs[u][:, :, :].rearrange("p s (h d) -> p (s h) d", d=HD), heads,
                                            q_max[:, u, :].rearrange("p (h o) -> p h o", o=1).broadcast_to([128, S * H, HD]),
                                            ALU.add).then_inc(lin_sub[u], 1)
                if kind == "lin_v":
                    wait_filled(dve, step, b)
                    nc.vector.tensor_tensor(l_v[u][:, :, :], by_seq(ps[:, 0:N]), rows[:, 1, :, :].broadcast_to([128, S, D]), ALU.add)\
                        .then_inc(drained[b], 1)
                if kind == "lin_turn":
                    dve.wait_ge(lin_exp[u], 1)
                    link(nc.vector.tensor_reduce(q_sum[:, u, :], l_e[u][:, 0, :, :].rearrange("p s (h d) -> p (s h) d", d=HD), AX.X, ALU.add))
                    nc.vector.reciprocal(q_inv[:, u, :], q_sum[:, u, :])
                    link(nc.vector.reciprocal(k_inv[:, u, :], k_sum[:, u, :]))
                if kind == "lin_ctx":
                    wait_filled(dve, step, b)
                    for s in range(S):
                        last = nc.vector.scalar_tensor_tensor(l_ctx[u][:, s, :], ps[:, s * D:(s + 1) * D], k_inv[:, u, s:s + 1], blocks,
                                                              ALU.mult, ALU.mult)
                    last.then_inc(drained[b], 1)
                if kind == "lin_y":
                    wait_filled(dve, step, b)
                    nc.vector.tensor_tensor(l_y[u][:, :, :].rearrange("p s (h d) -> p (s h) d", d=HD),
                                            ps[:, 0:N].rearrange("p (h d) -> p h d", d=HD),
                                            q_inv[:, u, :].rearrange("p (h o) -> p h o", o=1).broadcast_to([128, S * H, HD]),
                                            ALU.mult).then_inc(drained[b], 1)
                    wait_done(dve, step, b)
                    statistics(u, "1s", row_source(u, "1s"))
                if kind == "turned" and arg == "1s":
                    dve.wait_ge(lin_tanh[u], 1)
                    nc.vector.scalar_tensor_tensor(l_hs[u][:, :, :], l_t[u][:, :, :], 1.0, hT[u][:, :, :], ALU.add, ALU.mult)\
                        .then_inc(lin_silu[u], 1)

            for t, steps in slots():
                if 0 <= t < NGROUPS:
                    maxima(t)
                if 2 <= t < NGROUPS + 2:
                    turned_out(t - 2)
                if t >= 5 and (t - 5) % NG == 0 and (t - 5) // NG < NSEQ:
                    inverse((t - 5) // NG)
                if t >= 7 and (t - 7) % NG == 0 and (t - 7) // NG < NSEQ:
                    normalise((t - 7) // NG)
                for step in steps:
                    dense(step)

        @block.tensor
        def _(pe):
            def scores(g):
                layer, u, s, j = group(g)
                if j == 0:
                    pe.wait_ge(qk_ready[u], att_no(layer) + 1)
                if g >= 2:
                    pe.wait_ge(probs_ready, g - 1)
                ps = ps_scores[g % 2]
                last = nc.tensor.matmul(ps[:, :], q_strip[u][:, s, j, :], k_head[u][:, s, :, :].rearrange("p h t -> p (h t)"),
                                        start=True, stop=layer != 3)
                if layer == 3:
                    pe.wait_ge(cond_ready, 5)
                    last = nc.tensor.matmul(ps[:, :].rearrange("p (h t) -> p h t", h=GH), first_row[:, :],
                                            masked[:, S * u + s, :, :].broadcast_to([128, GH, T]), start=False, stop=True)
                last.then_inc(scores_ready, 1)

            def turn(g):
                pe.wait_ge(probs_ready, g + 1)
                if g >= 2:
                    pe.wait_ge(turned_read, g - 1)
                for i in range(GH):
                    last = nc.tensor.transpose(ps_turned[g % 2][:, i * T:(i + 1) * T], probs[:, g % 4, i, :], ident)
                last.then_inc(turned_ready, 1)

            def values(q):
                layer, u, s, _ = group(q * NG)
                pe.wait_ge(turned_read, NG * (q + 1))
                wait_written(pe, u, "v", layer)
                if q >= 1:
                    pe.wait_ge(att_read, q)
                for i in range(GH):
                    for j in range(NG):
                        h = GH * j + i
                        nc.tensor.matmul(ps_att[32 * j:32 * j + 32, 0:T], v_pad[u][:, s, h, :], probsT[:, q % 2, h, :],
                                         start=i == 0, stop=i == GH - 1)
                pe.wait_ge(rden_ready, q + 1)
                nc.tensor.transpose(ps_att[:, T:2 * T], rden_wide[:, q % 2, :, :].rearrange("p h d -> p (h d)"), ident)\
                    .then_inc(att_ready, 1)

            def dense(step):
                _, u, kind, arg, banks = step
                for b in banks:
                    wait_free(pe, step, b)
                b = banks[0] if banks else None
                ps = ps_dense[b] if banks else None
                flat = lambda tile: tile.rearrange("p s t -> p (s t)")
                h_flat = flat(hT[u][:, :, :])

                def mm(out, lhsT, rhs, start=True, stop=True):
                    return nc.tensor.matmul(out, lhsT, rhs, start=start, stop=stop)

                if kind == "cond":
                    pe.wait_ge(silu_ready, 1)
                    name = f"cond{arg}"
                    wait_weights(pe, name)
                    rhs = vec[:, VCOL["c"]] if arg[0] == "2" else sil[:, :]
                    for i in range(6 if arg == "0" else 2):
                        last = mm(ps[:, i * B:(i + 1) * B], wcol(name, i), rhs)
                    if arg == "2a":
                        last = mm(ps[:, 2 * B:2 * B + 1], wcol("o2"), vcol("bv2"))
                    last.then_inc(filled[b], 1)
                if kind == "enter":
                    pe.wait_ge(x_loaded, 16)
                    pe.wait_ge(const_loaded, 16)
                    for s in range(S):
                        last = nc.tensor.transpose(ps[:, s * T:(s + 1) * T], x_tok[:, S * u + s, :], ident)
                    last.then_inc(filled[b], 1)
                if kind == "stats" and banks:
                    pe.wait_ge(x_ready[u], BEFORE_NORM[arg])
                    for s in range(S):
                        last = nc.tensor.transpose(ps[:, s * T:(s + 1) * T], xT[u][:, s, :], ident)
                    last.then_inc(filled[b], 1)
                if kind == "turned":
                    if arg in ("0a", "1s"):
                        pe.wait_ge(xhat_ready[u], 1 if arg == "0a" else 2)
                    else:
                        wait_written(pe, u, "stats", arg)
                    for s in range(S):
                        last = nc.tensor.transpose(ps[:, s * T:(s + 1) * T], xhat[u][:, s, :], ident)
                    last.then_inc(filled[b], 1)
                if kind == "qk":
                    wait_written(pe, u, "turned", f"{arg}a")
                    wait_weights(pe, f"q{arg}")
                    mm(ps[:, 0:N], wcol(f"q{arg}"), h_flat)
                    mm(ps[:, N:2 * N], wcol(f"k{arg}"), h_flat).then_inc(filled[b], 1)
                if kind in ("v", "lin_v"):
                    for s in range(S):
                        last = mm(ps[:, s * D:(s + 1) * D], hT[u][:, s, :], wcol(f"v{arg}"))
                    last.then_inc(filled[b], 1)
                if kind == "out":
                    pe.wait_ge(att_read, B * att_no(arg) + S * (u + 1))
                    wait_weights(pe, f"o{arg}")
                    mm(ps[:, 0:N], wcol(f"o{arg}"), flat(att[u][:, :, :])).then_inc(filled[b], 1)
                if kind == "up":
                    wait_written(pe, u, "turned", f"{arg}m")
                    wait_weights(pe, f"up{arg}")
                    for c in range(FC):
                        last = mm(ps_dense[banks[c // 2]][:, (c % 2) * N:(c % 2 + 1) * N], wcol(f"up{arg}", c), h_flat)
                        if c % 2:
                            last.then_inc(filled[banks[c // 2]], 1)
                if kind == "gated":
                    wait_written(pe, u, "turned", "3m")
                    wait_weights(pe, "up3")
                    mm(ps[:, 0:N], wcol("up3", arg), h_flat)
                    mm(ps[:, N:2 * N], wcol("up3", FC + arg), h_flat).then_inc(filled[b], 1)
                if kind == "down":
                    if arg == 3:
                        for c in range(FC):
                            wait_written(pe, u, "gated", c)
                    else:
                        wait_written(pe, u, "up", arg)
                    for c in range(FC):
                        last = mm(ps[:, 0:N], wcol(f"down{arg}", c), hid[u][:, c, :], start=c == 0, stop=c == FC - 1)
                    last.then_inc(filled[b], 1)
                if kind == "lin_qk":
                    wait_written(pe, u, "turned", "1a")
                    wait_weights(pe, "q1")
                    for s in range(S):
                        mm(ps[:, s * D:(s + 1) * D], hT[u][:, s, :], wcol("q1"))
                    mm(ps[:, N:2 * N], wcol("k1"), h_flat).then_inc(filled[b], 1)
                if kind == "lin_turn":
                    pe.wait_ge(lin_exp[u], 1)
                    for i in range(2 * S):
                        last = nc.tensor.transpose(ps[:, i * T:(i + 1) * T], l_e[u][:, i // S, i % S, :], ident)
                    last.then_inc(filled[b], 1)
                if kind == "lin_ctx":
                    wait_written(pe, u, "lin_turn", 1)
                    wait_written(pe, u, "lin_v", 1)
                    for s in range(S):
                        last = mm(ps[:, s * D:(s + 1) * D], l_eT[u][:, (S + s) * T:(S + s + 1) * T], l_v[u][:, s, :])
                    last.then_inc(filled[b], 1)
                if kind == "lin_y":
                    wait_written(pe, u, "lin_ctx", 1)
                    for s in range(S):
                        last = mm(ps[:, s * D:(s + 1) * D], l_eT[u][:, s * T:(s + 1) * T], l_ctx[u][:, s, :])
                    last.then_inc(filled[b], 1)
                if kind == "lin_out":
                    pe.wait_ge(lin_silu[u], 1)
                    mm(ps[:, 0:N], wcol("o1"), flat(l_hs[u][:, :, :])).then_inc(filled[b], 1)
                if kind == "leave":
                    pe.wait_ge(x_ready[u], len(SUMS))
                    for s in range(S):
                        last = nc.tensor.transpose(ps[:, s * T:(s + 1) * T], xT[u][:, s, :], ident)
                    last.then_inc(filled[b], 1)

            for t, steps in slots():
                if 0 <= t < NGROUPS:
                    scores(t)
                if 2 <= t < NGROUPS + 2:
                    turn(t - 2)
                if t >= 6 and (t - 6) % NG == 0 and (t - 6) // NG < NSEQ:
                    values((t - 6) // NG)
                for step in steps:
                    dense(step)


def kernel(**inputs):
    import numpy as np
    import concourse.bacc as bacc
    from concourse.bass_utils import run_bass_kernel_spmd

    def arr(name):
        return np.asarray(inputs[name])

    def cols(name):
        return arr(name).reshape(-1, 128).T

    def chunked(m):
        return m.reshape(-1, 128, m.shape[1]).transpose(1, 0, 2).reshape(128, -1)

    def per_query_head(m):
        return np.repeat(m.reshape(HD // 2, HD, D), GH, axis=0).reshape(D, D)

    qkv3 = arr("L3_cond_qkv_w")
    weights = {
        "cond0": arr("L0_cond_wc").T, "q0": arr("L0_cond_wq").T, "k0": per_query_head(arr("L0_cond_wk")).T,
        "v0": per_query_head(arr("L0_cond_wv")).T, "o0": arr("L0_cond_wo").T, "up0": arr("L0_cond_w1").T,
        "down0": chunked(arr("L0_cond_w2").T),
        "cond1": arr("L1_cond_emb_W"), "q1": arr("L1_cond_Wq"), "k1": arr("L1_cond_Wk"), "v1": arr("L1_cond_Wv"),
        "o1": arr("L1_cond_out_W"),
        "cond2a": arr("L2_cond_wt_attn"), "cond2m": arr("L2_cond_wt_ffn"), "q2": arr("L2_cond_wq"), "k2": arr("L2_cond_wk"),
        "v2": arr("L2_cond_wv"), "o2": arr("L2_cond_wo"), "up2": arr("L2_cond_w1"), "down2": chunked(arr("L2_cond_w2")),
        "cond3": np.concatenate([arr("L3_cond_scale_w").T, arr("L3_cond_shift_w").T], axis=1),
        "q3": qkv3[0:D].T, "k3": qkv3[D:2 * D].T, "v3": qkv3[2 * D:].T, "o3": arr("L3_cond_proj_w").T,
        "up3": arr("L3_cond_mlp_w1").T, "down3": chunked(arr("L3_cond_mlp_w2").T),
    }
    vectors = {
        "c": arr("cond_1024").T, "bc0": cols("L0_cond_bc"), "bup0": cols("L0_cond_b1"), "bdown0": cols("L0_cond_b2"),
        "g1": cols("L1_cond_norm_g"), "b1": cols("L1_cond_norm_b"), "bk1": cols("L1_cond_bk"), "bcond1": cols("L1_cond_emb_b"),
        "gs1": cols("L1_cond_sn_g"), "bs1": cols("L1_cond_sn_b"), "bo1": cols("L1_cond_out_b"),
        "g2a": cols("L2_cond_ln1_w"), "b2a": cols("L2_cond_ln1_b"), "g2m": cols("L2_cond_ln2_w"), "b2m": cols("L2_cond_ln2_b"),
        "bq2": cols("L2_cond_bq"), "bk2": cols("L2_cond_bk"), "bv2": cols("L2_cond_bv"), "bo2": cols("L2_cond_bo"),
        "bcond2a": cols("L2_cond_bt_attn"), "bcond2m": cols("L2_cond_bt_ffn"), "bup2": cols("L2_cond_b1"),
        "bdown2": cols("L2_cond_b2"), "g3": cols("L3_cond_norm_w"),
        "bcond3": np.concatenate([cols("L3_cond_scale_b"), cols("L3_cond_shift_b")], axis=1),
        "bo3": cols("L3_cond_proj_b"), "bup3": cols("L3_cond_mlp_b1"), "bdown3": cols("L3_cond_mlp_b2"),
    }
    head = np.arange(D) // HD
    const = np.concatenate([
        np.eye(D), head[:, None] == head[None, :], head[:, None] % GH == np.arange(GH)[None, :],
        head[:, None] // GH == np.arange(NG)[None, :], np.full((D, S), -0.5),
    ], axis=1).astype(np.float32)
    arrays = {
        "x": np.ascontiguousarray(arr("x")),
        "vectors": np.ascontiguousarray(np.concatenate([vectors[n] for n, _ in VECTORS], axis=1)),
        "weights": np.ascontiguousarray(np.concatenate([weights[n] for n, _ in WEIGHTS], axis=1)),
        "row_biases": np.concatenate([arr("L1_cond_bq"), arr("L1_cond_bv")]),
        "mask": np.ascontiguousarray(arr("mask_BxS_ik0")).reshape(-1),
        "constants": const,
    }
    nc = bacc.Bacc("TRN2", target_bir_lowering=False, num_devices=1)
    args = [nc.dram_tensor(n, a.shape, mybir.dt.from_np(a.dtype), kind="ExternalInput").ap() for n, a in arrays.items()]
    out = nc.dram_tensor("out", (B, T, D), F32, kind="ExternalOutput").ap()
    build(nc, *args, out)
    r = run_bass_kernel_spmd(nc, [arrays], core_ids=[0])
    return r.results[0]["out"]
```

```python
from contextlib import ExitStack

import concourse.bass as bass
from concourse import mybir

F32 = mybir.dt.float32
F32R = mybir.dt.float32r
I32 = mybir.dt.int32
ALU = mybir.AluOpType
ACT = mybir.ActivationFunctionType
AX = mybir.AxisListType

B, T, D = 8, 128, 128
H, HD = 16, 8
GH = 4
NG = H // GH
U = 4
S = B // U
N = S * T
F = 512
FC = F // D
NATT = 3
NGROUPS = NATT * B * NG
NSEQ = NATT * B
NSC, NTU, NDENSE = 3, 1, 3
SCORES, MAXIMA, TURN, TURNED_OUT = -1, -1, 2, 2
INVERSE, VALUES, INVERSE_SUMS, NORMALISE = 5, 6, 7, 8
ACT_LATER = {}
DVE_LATER = {"gated": 0.5}

TERMS = 3
ROWS = 4
PARTS = 16 * 4
STACKING = 16 * (1 + GH)
MASKED = -2.0 ** 100

WEIGHTS = [
    ("cond0", 6 * D), ("q0", D), ("k0", D), ("v0", D), ("o0", D), ("up0", F), ("down0", F),
    ("cond1", 2 * D), ("q1", D), ("k1", D), ("v1", D), ("o1", D),
    ("cond2a", 2 * D), ("cond2m", 2 * D), ("q2", D), ("k2", D), ("v2", D), ("o2", D), ("up2", F), ("down2", F),
    ("cond3", 2 * D), ("q3", D), ("k3", D), ("v3", D), ("o3", D), ("up3", 2 * F), ("down3", F),
]
LOADS = [("cond0",), ("q0", "k0", "v0"), ("o0", "up0", "down0"), ("cond1", "q1", "k1", "v1", "o1"),
         ("cond2a", "cond2m", "q2", "k2", "v2", "o2"), ("up2", "down2"), ("cond3", "q3", "k3", "v3", "o3"),
         ("up3", "down3")]
VECTORS = [
    ("c", B), ("bc0", 6), ("bup0", FC), ("bdown0", 1),
    ("g1", 1), ("b1", 1), ("bk1", 1), ("bcond1", 2), ("gs1", 1), ("bs1", 1), ("bo1", 1),
    ("g2a", 1), ("b2a", 1), ("g2m", 1), ("b2m", 1), ("bq2", 1), ("bk2", 1), ("bv2", 1), ("bo2", 1),
    ("bcond2a", 2), ("bcond2m", 2), ("bup2", FC), ("bdown2", 1),
    ("g3", 1), ("bcond3", 2), ("bo3", 1), ("bup3", 2 * FC), ("bdown3", 1),
]
CONST = 2 * D + S
NORMS = ["0a", "0m", "1a", "1s", "2a", "2m", "3a", "3m"]
EPS = 1e-5
EPS3 = 1e-6


def columns(items):
    at, out = 0, {}
    for name, n in items:
        out[name] = slice(at, at + n)
        at += n
    return out, at


WCOL, WTOTAL = columns(WEIGHTS)
VCOL, VTOTAL = columns(VECTORS)


def norm_steps(which):
    return [("stats", which), ("normed", which), ("turned", which)]


PHASES = [
    [("enter", 0), *norm_steps("0a"), ("qk", 0), ("v", 0)],
    [("out", 0), *norm_steps("0m"), ("up", 0), ("down", 0), *norm_steps("1a"), ("lin_qk", 1), ("lin_v", 1), ("lin_turn", 1),
     ("lin_ctx", 1), ("lin_y", 1), ("normed", "1s"), ("turned", "1s"), ("lin_out", 1), *norm_steps("2a"), ("qk", 2), ("v", 2)],
    [("out", 2), *norm_steps("2m"), ("up", 2), ("down", 2), *norm_steps("3a"), ("qk", 3), ("v", 3)],
    [("out", 3), *norm_steps("3m"), *[("gated", c) for c in range(FC)], ("down", 3), ("leave", 3)],
]
START = [-12, -11, -4, 5]
SPACING = [
    [1.5, 0.5, 1, 1, 1, 1],
    [0.72, 0.72, 0.72, 0.72, 0.72, 0.72, 0.9, 0.54, 0.72, 0.72, 0.72, 0.72, 0.72, 0.72, 0.72, 0.22, 0.72, 0.54, 0.9, 0.0, 0.72, 0.72],
    [1.4, 1.4, 1.4, 1.4, 1.4, 1.4, 1.4, 1.4, 1.4, 1.4, 1.4],
    [1.0, 1.2, 0.8, 1.0, 1.0, 1.0, 1.0, 1.0, 1.0, 1.0],
]
FIRSTS = [0, 4, 4.25, 4.5]
CONDITIONS = [("0", -9.5), ("1", 1.1), ("2a", 2.1), ("2m", 3.1), ("3", 4.1)]


def plan():
    steps = [(slot, 0, "cond", name) for name, slot in CONDITIONS]
    for u in range(U):
        for phase, kinds in enumerate(PHASES):
            slot = START[u] if phase == 0 else S * NG * (u + 1) + B * NG * (phase - 1) + FIRSTS[phase]
            for kind, gap in zip(kinds, SPACING[phase]):
                steps.append((slot, u, *kind))
                slot += gap
    steps.sort(key=lambda x: x[0])
    out, ring, held = [], list(range(NDENSE)), {}
    for step in steps:
        _, u, kind, which = step
        free = [b for b in ring if b not in held.values()]
        banks = tuple(free[:{"normed": 0, "up": 2, "stats": 0 if which == "0a" else 1}.get(kind, 1)])
        assert kind != "up" or len(banks) == 2
        for b in banks:
            ring.remove(b)
            ring.append(b)
        if kind == "stats" and banks:
            held[u] = banks[0]
        if kind == "normed":
            held.pop(u, None)
        out.append((*step, banks))
    return out


def build(nc, x_in, c_in, w_in, rows_in, mask_in, const_in, pads_in, parts, out):
    with ExitStack() as ctx:
        def sb(name, shape, dt=F32):
            return ctx.enter_context(nc.sbuf_tensor(name, shape, dt))

        def sem(name):
            return ctx.enter_context(nc.semaphore(name))

        def sems(name, n):
            return [sem(f"{name}{i}") for i in range(n)]

        w = sb("w", [128, WTOTAL])
        vec = sb("vec", [128, VTOTAL])
        rows = sb("rows", [128, 2, 1, D])
        mask_i = sb("mask_i", [128, B, T], I32)
        masked = sb("masked", [128, B, 1, T], F32R)
        const = sb("const", [128, CONST])
        ident = const[:, 0:D]
        blocks = const[:, D:2 * D]
        minus_half = const[:, 2 * D:CONST]

        x_tok = sb("x_tok", [128, B, D])
        y_tok = sb("y_tok", [128, B, D])

        def per_unit(name, shape, n=U, dt=F32):
            tiles = [sb(f"{name}{i}", shape, dt) for i in range(n)]
            return [tiles[u % n] for u in range(U)]

        xT = per_unit("xT", [128, S, T])
        xhat = per_unit("xhat", [128, S, D])
        hT = per_unit("hT", [128, S, T])
        qkT = per_unit("qkT", [128, 2, S, T], 2)
        qk_high = per_unit("qk_high", [128, 2, N], 2, F32R)
        qk_low = per_unit("qk_low", [128, 2, N], 2, F32R)
        q_stack = per_unit("q_stack", [128, NG, N], 2, F32R)
        k_stack = per_unit("k_stack", [128, NG, GH, N], 2, F32R)
        v_pad = per_unit("v_pad", [128, S, H, 32])
        att = per_unit("att", [128, S, T])
        scaled = per_unit("scaled", [128, S, T], 2)
        hid = per_unit("hid", [128, FC, N], 2)
        th = sb("th", [128, 2, N])
        half = sb("half", [128, 2, N])
        silu_g = sb("silu_g", [128, 2, N])
        bn = sb("bn", [128, U, S, 6])
        mv = sb("mv", [128, U, S, 2])
        base = sb("base", [128, U, S])
        rstd = sb("rstd", [128, U, S])
        l_q = per_unit("l_q", [128, S, D], 2)
        l_qs = per_unit("l_qs", [128, S, D], 2)
        l_k = per_unit("l_k", [128, S, T], 2)
        l_v = per_unit("l_v", [128, S, D], 2)
        l_e = per_unit("l_e", [128, 2, S, T], 2)
        l_eT = per_unit("l_eT", [128, 2 * S * T], 2)
        l_ctx = per_unit("l_ctx", [128, S, D], 2)
        l_y = per_unit("l_y", [128, S, D], 2)
        l_t = per_unit("l_t", [128, S, T], 2)
        l_hs = per_unit("l_hs", [128, S, T], 2)
        q_max = sb("q_max", [128, U, S * H])
        q_sum = sb("q_sum", [128, U, S * H])
        q_inv = sb("q_inv", [128, U, S * H])
        k_max = sb("k_max", [128, U, S])
        k_sum = sb("k_sum", [128, U, S])
        k_inv = sb("k_inv", [128, U, S])
        c_tanh = sb("c_tanh", [128, B])
        c_half = sb("c_half", [128, B])
        sil = sb("sil", [128, B])
        cnd = sb("cnd", [128, 14, B])
        tmp = sb("tmp", [128, 2, B])
        mod_a = sb("mod_a", [128, len(NORMS), B])
        mod_b = sb("mod_b", [128, len(NORMS), B])
        bq2_scaled = sb("bq2_scaled", [128, 1])
        bo2_full = sb("bo2_full", [128, 1])
        bup3_half = sb("bup3_half", [128, FC])
        probs = sb("probs", [128, 4, GH, T])
        probsT = sb("probsT", [128, 2, H, T])
        neg_max = sb("neg_max", [128, NGROUPS, GH])
        den = sb("den", [128, NSEQ, H])
        rden = sb("rden", [128, NSEQ, H, 1])
        rden_wide = sb("rden_wide", [128, 2, H, HD])
        rdenT = sb("rdenT", [128, 2, T])

        psum = [ctx.enter_context(nc.psum_tensor(f"ps{i}", [128, 512], F32)) for i in range(8)]
        ps_scores, ps_turned, ps_att, ps_dense = psum[0:NSC], psum[NSC:NSC + NTU], psum[7 - NDENSE], psum[8 - NDENSE:]

        x_loaded, vec_loaded, const_loaded, row_loaded = sem("x_loaded"), sem("vec_loaded"), sem("const_loaded"), sem("row_loaded")
        w_loaded = sems("w_loaded", len(LOADS))
        stored = sem("stored")
        c_tanh_ready, silu_ready = sem("c_tanh_ready"), sem("silu_ready")
        cond_ready = sem("cond_ready")
        filled = sems("filled", NDENSE)
        drained = sems("drained", NDENSE)
        x_ready = sems("x_ready", U)
        var_ready, rstd_ready, xhat_ready = sems("var_ready", U), sems("rstd_ready", U), sems("xhat_ready", U)
        split_high, split_low = sem("split_high"), sem("split_low")
        parts_stored, stacked = sems("parts_stored", 2), sems("stacked", 2)
        mask_ready = sem("mask_ready")
        v_cleared = sem("v_cleared")
        stack_cleared = sem("stack_cleared")
        pads_stored = sem("pads_stored")
        lin_sub, lin_exp = sems("lin_sub", U), sems("lin_exp", U)
        lin_tanh, lin_silu = sems("lin_tanh", U), sems("lin_silu", U)
        gate_halves = sem("gate_halves")
        y_ready = sem("y_ready")
        scores_ready, max_ready, probs_ready = sem("scores_ready"), sem("max_ready"), sem("probs_ready")
        turned_ready, turned_read = sem("turned_ready"), sem("turned_read")
        rden_ready, att_ready, rdenT_ready, att_read = sem("rden_ready"), sem("att_ready"), sem("rdenT_ready"), sem("att_read")
        dve_own = sem("dve_own")

        STEPS = plan()
        FIRST, LAST = int(STEPS[0][0]) - 1, int(STEPS[-1][0]) + 4
        step_of = {(s[1], s[2], s[3]): s for s in STEPS}
        before, fills, drains, last_of = {}, {}, {}, {}
        n_fill, n_drain = [0] * NDENSE, [0] * NDENSE
        SUMS = [("enter", 0), ("out", 0), ("down", 0), ("lin_out", 1), ("out", 2), ("down", 2), ("out", 3), ("down", 3)]
        BEFORE_NORM = {"0m": 2, "1a": 3, "2a": 4, "2m": 5, "3a": 6, "3m": 7}
        for s in STEPS:
            for b in s[4]:
                before[s, b] = last_of.get(b)
                last_of[b] = s
                n_fill[b] += 1
                fills[s, b] = n_fill[b]
                if (s[2], s[3]) not in SUMS and s[2] != "leave":
                    n_drain[b] += 1
                    drains[s, b] = n_drain[b]
        gated_no = {s: i for i, s in enumerate(x for x in STEPS if x[2] == "gated")}

        def slots(later={}):
            at = [(s[0] + later.get(s[2], later.get(s[2:4], 0)), s) for s in STEPS]
            at.sort(key=lambda x: x[0])
            for t in range(FIRST, LAST):
                yield t, [s for slot, s in at if int(slot - FIRST) + FIRST == t]

        def wait_done(eng, step, b):
            _, u, kind, arg, _ = step
            if (kind, arg) in SUMS:
                eng.wait_ge(x_ready[u], SUMS.index((kind, arg)) + 1)
            elif kind == "leave":
                eng.wait_ge(y_ready, u + 1)
            else:
                eng.wait_ge(drained[b], drains[step, b])

        def wait_written(eng, u, kind, arg):
            step = step_of[u, kind, arg]
            for b in step[4]:
                wait_done(eng, step, b)

        def wait_free(eng, step, b):
            if before[step, b] is not None:
                wait_done(eng, before[step, b], b)

        def wait_filled(eng, step, b):
            eng.wait_ge(filled[b], fills[step, b])

        def wait_weights(eng, name):
            eng.wait_ge(w_loaded[next(i for i, names in enumerate(LOADS) if name in names)], 16)

        def vcol(name, i=0):
            at = VCOL[name].start + i
            return vec[:, at:at + 1]

        def wcol(name, i=0):
            at = WCOL[name].start + i * D
            return w[:, at:at + D]

        def att_no(layer):
            return (0, 2, 3).index(layer)

        def group(g):
            a, r = divmod(g, B * NG)
            u, r = divmod(r, S * NG)
            return (0, 2, 3)[a], u, r // NG, r % NG

        def done(t, after):
            q, r = divmod(t - after, NG)
            return q if r == 0 and 0 <= q < NSEQ else None

        def by_seq(tile):
            return tile.rearrange("p (s t) -> p s t", s=S)

        NO = {n: i for i, n in enumerate(NORMS)}
        block = ctx.enter_context(nc.Block())

        @block.sync
        def _(sp):
            sp.dma_start(vec[:, :], c_in).then_inc(vec_loaded, 16)
            sp.dma_start(x_tok[:, :, :], x_in.rearrange("b t d -> t b d")).then_inc(x_loaded, 16)
            for i in range(1, len(LOADS), 2):
                cols = slice(WCOL[LOADS[i][0]].start, WCOL[LOADS[i][-1]].stop)
                sp.dma_start(w[:, cols], w_in[:, cols]).then_inc(w_loaded[i], 16)
                if i == 1:
                    for ring in range(2):
                        sp.dma_start(parts[ring, :, :, TERMS, :], pads_in).then_inc(pads_stored, 16)
            sp.wait_ge(pads_stored, 16 * 2)

            def stack(u, layer):
                n = U * att_no(layer) + u
                scratch = parts[n % 2]
                high, low = qk_high[u][:, :, :].bitcast(F32), qk_low[u][:, :, :].bitcast(F32)
                if n >= 2:
                    sp.wait_ge(stacked[n % 2], STACKING * (n // 2))
                sp.wait_ge(split_high, n + 1)
                for a, terms in ((0, slice(0, 2)), (1, slice(0, 3, 2))):
                    sp.dma_start(scratch[a, :, terms, :], high[:, a:a + 1, :].broadcast_to([128, 2, N])).then_inc(parts_stored[n % 2], 16)
                if layer == 3:
                    sp.wait_ge(mask_ready, 1)
                    sp.dma_start(scratch[1].rearrange("(h d) t n -> h d t n", d=HD)[:, 0, TERMS, :],
                                 masked[0:H, S * u:S * (u + 1), 0, :].rearrange("p s t -> p (s t)").bitcast(F32))\
                        .then_inc(parts_stored[n % 2], 16)
                sp.wait_ge(split_low, n + 1)
                for a, t in ((0, 2), (1, 1)):
                    sp.dma_start(scratch[a, :, t, :], low[:, a, :]).then_inc(parts_stored[n % 2], 16)
                if n < 2:
                    sp.wait_ge(stack_cleared, n + 1)
                else:
                    sp.wait_ge(scores_ready, S * NG * (n - 1))
                sp.wait_ge(parts_stored[n % 2], PARTS * (n // 2 + 1) + 16 * (layer == 3) * (u // 2 + 1))
                rows_of = scratch.rearrange("a (j r) t n -> a (r t) j n", j=NG)
                sp.dma_start(q_stack[u][:, :, :].bitcast(F32), rows_of[0]).then_inc(stacked[n % 2], 16)
                for i in range(GH):
                    strip = slice(32 * i, 32 * (i + 1))
                    sp.dma_start(k_stack[u][strip, :, i, :].bitcast(F32), rows_of[1, strip]).then_inc(stacked[n % 2], 16)

            for _, steps in slots():
                for _, u, kind, arg, _ in steps:
                    if kind == "qk":
                        stack(u, arg)
                    if kind == "leave":
                        sp.wait_ge(y_ready, u + 1)
                        sp.dma_start(out.rearrange("b t d -> t b d")[:, u * S:(u + 1) * S, :],
                                     y_tok[:, u * S:(u + 1) * S, :]).then_inc(stored, 16)
            sp.wait_ge(stored, 16 * U)

        @block.gpsimd
        def _(pool):
            pool.dma_start(rows[:, :, :, :].rearrange("p a o d -> p (a o d)"), rows_in.partition_broadcast(128)).then_inc(row_loaded, 16)
            pool.dma_start(mask_i[:, :, :].rearrange("p b t -> p (b t)"), mask_in.partition_broadcast(128)).then_inc(row_loaded, 16)

            def power(u, which):
                pool.wait_ge(var_ready[u], NO[which] + 1)
                nc.gpsimd.tensor_tensor(rstd[:, u, :], base[:, u, :], minus_half, ALU.pow).then_inc(rstd_ready[u], 1)

            def split(step):
                _, u, _, layer, (b,) = step
                n = U * att_no(layer) + u
                if n >= 2:
                    pool.wait_ge(parts_stored[n % 2], PARTS * (n // 2))
                wait_done(pool, step, b)
                both = qkT[u][:, :, :, :].rearrange("p a s t -> p a (s t)")
                nc.gpsimd.tensor_scalar(qk_high[u][:, :, :], both, 1.0, None, ALU.mult).then_inc(split_high, 1)
                pool.wait_ge(split_high, n + 1)
                nc.gpsimd.tensor_tensor(qk_low[u][:, :, :], both, qk_high[u][:, :, :].bitcast(F32), ALU.subtract)\
                    .then_inc(split_low, 1)

            def clear_stack(u):
                nc.gpsimd.memset(k_stack[u][:, :, :, :].bitcast(F32), 0.0).then_inc(stack_cleared, 1)

            clear_stack(0)
            pool.wait_ge(const_loaded, 16)
            for t, steps in slots():
                for step in steps:
                    if step[2] == "stats":
                        power(step[1], step[3])
                    if step[2] == "lin_y":
                        power(step[1], "1s")
                    if step[2] == "qk":
                        split(step)
                        if step[1:] == (0, "qk", 0, step[4]):
                            clear_stack(1)

        @block.scalar
        def _(act):
            cols = slice(WCOL[LOADS[0][0]].start, WCOL[LOADS[0][-1]].stop)
            act.dma_start(w[:, cols], w_in[:, cols]).then_inc(w_loaded[0], 16)
            act.dma_start(const[:, :], const_in).then_inc(const_loaded, 16)
            for i in range(2, len(LOADS), 2):
                cols = slice(WCOL[LOADS[i][0]].start, WCOL[LOADS[i][-1]].stop)
                act.dma_start(w[:, cols], w_in[:, cols]).then_inc(w_loaded[i], 16)
            act.wait_ge(vec_loaded, 16)
            nc.scalar.activation(c_tanh[:, :], vec[:, VCOL["c"]], ACT.Tanh, scale=0.5).then_inc(c_tanh_ready, 1)

            def exps(g):
                act.wait_ge(max_ready, g + 1)
                if g >= 4:
                    act.wait_ge(turned_ready, g - 3)
                for i in range(GH):
                    last = nc.scalar.activation(probs[:, g % 4, i, :], ps_scores[g % NSC][:, i * T:(i + 1) * T], ACT.Exp,
                                                bias=neg_max[:, g, i:i + 1],
                                                accum_out=den[:, g // NG, GH * (g % NG) + i:GH * (g % NG) + i + 1])
                last.then_inc(probs_ready, 1)

            def inverse_sums(q):
                act.wait_ge(att_ready, q + 1)
                nc.scalar.activation(rdenT[:, q % 2, :], ps_att[:, T:2 * T], ACT.Copy).then_inc(rdenT_ready, 1)

            def dense(step):
                _, u, kind, arg, banks = step
                ps = [ps_dense[b] for b in banks]
                if kind == "enter":
                    wait_filled(act, step, banks[0])
                    nc.scalar.activation(xT[u][:, :, :], by_seq(ps[0][:, 0:N]), ACT.Copy).then_inc(x_ready[u], 1)
                if kind == "turned":
                    wait_filled(act, step, banks[0])
                    act.wait_ge(cond_ready, {"0": 1, "1": 2, "2": 4, "3": 5}[arg[0]])
                    for s in range(S):
                        i = S * u + s
                        last = nc.scalar.activation(hT[u][:, s, :], ps[0][:, s * T:(s + 1) * T], ACT.Identity,
                                                    scale=mod_a[:, NO[arg], i:i + 1], bias=mod_b[:, NO[arg], i:i + 1])
                    last.then_inc(drained[banks[0]], 1)
                    if arg == "1s":
                        wait_done(act, step, banks[0])
                        nc.scalar.activation(l_t[u][:, :, :], hT[u][:, :, :], ACT.Tanh).then_inc(lin_tanh[u], 1)
                if kind == "qk":
                    n = U * att_no(arg) + u
                    if n >= 2:
                        act.wait_ge(split_low, n - 1)
                    wait_filled(act, step, banks[0])
                    q, k = by_seq(ps[0][:, 0:N]), by_seq(ps[0][:, N:2 * N])
                    if arg == 2:
                        nc.scalar.activation(qkT[u][:, 0, :, :], q, ACT.Identity, scale=HD ** -0.5, bias=bq2_scaled[:, :])
                        last = nc.scalar.activation(qkT[u][:, 1, :, :], k, ACT.Identity, bias=vcol("bk2"))
                    else:
                        nc.scalar.activation(qkT[u][:, 0, :, :], q, ACT.Copy, scale=HD ** -0.5)
                        last = nc.scalar.activation(qkT[u][:, 1, :, :], k, ACT.Copy)
                    last.then_inc(drained[banks[0]], 1)
                if kind == "up":
                    for h in range(2):
                        wait_filled(act, step, banks[h])
                        for c in (2 * h, 2 * h + 1):
                            last = nc.scalar.activation(hid[u][:, c, :], ps[h][:, (c % 2) * N:(c % 2 + 1) * N], ACT.Gelu,
                                                        bias=vcol(f"bup{arg}", c))
                        last.then_inc(drained[banks[h]], 1)
                if kind == "gated":
                    n = gated_no[step]
                    wait_filled(act, step, banks[0])
                    if n >= 2:
                        prev = list(gated_no)[n - 2]
                        wait_done(act, prev, prev[4][0])
                    nc.scalar.activation(th[:, n % 2, :], ps[0][:, 0:N], ACT.Tanh, scale=0.5, bias=bup3_half[:, arg:arg + 1])
                    nc.scalar.activation(half[:, n % 2, :], ps[0][:, 0:N], ACT.Identity, scale=0.5,
                                         bias=bup3_half[:, arg:arg + 1]).then_inc(gate_halves, 1)
                if kind == "lin_qk":
                    act.wait_ge(lin_sub[u], 1)
                    nc.scalar.activation(l_e[u][:, 0, :, :], l_qs[u][:, :, :], ACT.Exp)
                    for s in range(S):
                        last = nc.scalar.activation(l_e[u][:, 1, s, :], l_k[u][:, s, :], ACT.Exp, bias=k_max[:, u, s:s + 1],
                                                    accum_out=k_sum[:, u, s:s + 1])
                    last.then_inc(lin_exp[u], 1)
                if kind == "lin_turn":
                    wait_filled(act, step, banks[0])
                    nc.scalar.activation(l_eT[u][:, :], ps[0][:, :], ACT.Copy).then_inc(drained[banks[0]], 1)
                if kind == "leave":
                    wait_filled(act, step, banks[0])
                    nc.scalar.activation(y_tok[:, u * S:(u + 1) * S, :], by_seq(ps[0][:, 0:N]), ACT.Copy).then_inc(y_ready, 1)

            for t, steps in slots(ACT_LATER):
                if 0 <= t < NGROUPS:
                    exps(t)
                if done(t, INVERSE_SUMS) is not None:
                    inverse_sums(done(t, INVERSE_SUMS))
                for step in steps:
                    dense(step)

        @block.vector
        def _(dve):
            own = [0]

            def link(ins):
                own[0] += 1
                ins.then_inc(dve_own, 1)
                dve.wait_ge(dve_own, own[0])

            dve.wait_ge(vec_loaded, 16)
            link(nc.vector.tensor_scalar(c_half[:, :], vec[:, VCOL["c"]], 0.5, None, ALU.mult))
            dve.wait_ge(c_tanh_ready, 1)
            nc.vector.scalar_tensor_tensor(sil[:, :], c_tanh[:, :], 1.0, c_half[:, :], ALU.add, ALU.mult).then_inc(silu_ready, 1)
            nc.vector.tensor_scalar(bq2_scaled[:, :], vcol("bq2"), HD ** -0.5, None, ALU.mult)
            nc.vector.tensor_scalar(bup3_half[:, :], vec[:, VCOL["bup3"].start:VCOL["bup3"].start + FC], 0.5, None, ALU.mult)

            def maxima(g):
                dve.wait_ge(scores_ready, g + 1)
                nc.vector.tensor_reduce(neg_max[:, g, :], ps_scores[g % NSC][:, :].rearrange("p (h k) -> p h k", h=GH), AX.X,
                                        ALU.max, negate=True).then_inc(max_ready, 1)

            def turned_out(g):
                dve.wait_ge(turned_ready, g + 1)
                q = g // NG
                if q >= 2 and g % NG == 0:
                    dve.wait_ge(att_ready, q - 1)
                nc.vector.tensor_copy(probsT[:, q % 2, GH * (g % NG):GH * (g % NG + 1), :].rearrange("p h t -> p (h t)"),
                                      ps_turned[g % NTU][:, :]).then_inc(turned_read, 1)

            def inverse(q):
                dve.wait_ge(probs_ready, NG * (q + 1))
                link(nc.vector.reciprocal(rden[:, q, :, 0], den[:, q, :]))
                if q >= 2:
                    dve.wait_ge(att_ready, q - 1)
                nc.vector.tensor_copy(rden_wide[:, q % 2, :, :], rden[:, q, :, :].broadcast_to([128, H, HD])).then_inc(rden_ready, 1)

            def normalise(q):
                _, u, s, _ = group(q * NG)
                dve.wait_ge(rdenT_ready, q + 1)
                nc.vector.tensor_tensor(att[u][:, s, :], ps_att[:, 0:T], rdenT[:, q % 2, :], ALU.mult).then_inc(att_read, 1)

            def statistics(u, which, src):
                for s in range(S):
                    last = nc.vector.bn_stats(bn[:, u, s, :], src(s))
                link(last)
                for s in range(S):
                    last = nc.vector.bn_aggr(mv[:, u, s, :], bn[:, u, s, :])
                link(last)
                if which[0] == "3":
                    link(nc.vector.tensor_tensor(base[:, u, :], mv[:, u, :, 0], mv[:, u, :, 0], ALU.mult))
                    link(nc.vector.tensor_tensor(base[:, u, :], base[:, u, :], mv[:, u, :, 1], ALU.add))
                    nc.vector.tensor_scalar(base[:, u, :], base[:, u, :], EPS3 * EPS3, None, ALU.max).then_inc(var_ready[u], 1)
                else:
                    nc.vector.tensor_scalar(base[:, u, :], mv[:, u, :, 1], EPS, None, ALU.add).then_inc(var_ready[u], 1)

            def row_source(u, which):
                if which == "0a":
                    return lambda s: x_tok[:, S * u + s, :]
                if which == "1s":
                    return lambda s: l_y[u][:, s, :]
                (b,) = step_of[u, "stats", which][4]
                return lambda s: ps_dense[b][:, s * T:(s + 1) * T]

            def add_scaled(step, name, gate):
                _, u, _, _, (b,) = step
                for s in range(S):
                    last = nc.vector.tensor_scalar(scaled[u][:, s, :], ps_dense[b][:, s * T:(s + 1) * T], vcol(name),
                                                   gate(S * u + s), ALU.add, ALU.mult)
                link(last)
                nc.vector.tensor_tensor(xT[u][:, :, :], xT[u][:, :, :], scaled[u][:, :, :], ALU.add).then_inc(x_ready[u], 1)

            def condition(step):
                _, _, _, arg, (b,) = step
                wait_filled(dve, step, b)
                ps = ps_dense[b]

                def plus_bias(first, n, name):
                    nc.vector.tensor_tensor(cnd[:, first:first + n, :], ps[:, 0:n * B].rearrange("p (i b) -> p i b", i=n),
                                            vec[:, VCOL[name]].rearrange("p (i o) -> p i o", o=1).broadcast_to([128, n, B]),
                                            ALU.add).then_inc(drained[b], 1)
                    wait_done(dve, step, b)

                def modulate(which, scale, shift, g, bias):
                    nc.vector.tensor_scalar(mod_a[:, NO[which], :], cnd[:, scale, :], 1.0, vcol(g), ALU.add, ALU.mult)
                    link(nc.vector.tensor_scalar(tmp[:, 0, :], cnd[:, scale, :], 1.0, vcol(bias), ALU.add, ALU.mult))
                    return nc.vector.tensor_tensor(mod_b[:, NO[which], :], tmp[:, 0, :], cnd[:, shift, :], ALU.add)

                if arg == "0":
                    plus_bias(0, 6, "bc0")
                    for which, i in (("0a", 0), ("0m", 3)):
                        nc.vector.tensor_scalar(mod_a[:, NO[which], :], cnd[:, i + 1, :], 1.0, None, ALU.add)
                        last = nc.vector.tensor_copy(mod_b[:, NO[which], :], cnd[:, i, :])
                    last.then_inc(cond_ready, 1)
                if arg == "1":
                    plus_bias(6, 2, "bcond1")
                    nc.vector.tensor_copy(mod_a[:, NO["1a"], :], vcol("g1").broadcast_to([128, B]))
                    nc.vector.tensor_copy(mod_b[:, NO["1a"], :], vcol("b1").broadcast_to([128, B]))
                    link(modulate("1s", 6, 7, "gs1", "bs1"))
                    for m in (mod_a, mod_b):
                        last = nc.vector.tensor_scalar(m[:, NO["1s"], :], m[:, NO["1s"], :], 0.5, None, ALU.mult)
                    last.then_inc(cond_ready, 1)
                if arg == "2a":
                    nc.vector.tensor_tensor(bo2_full[:, :], ps[:, 2 * B:2 * B + 1], vcol("bo2"), ALU.add)
                    plus_bias(8, 2, "bcond2a")
                    modulate("2a", 9, 8, "g2a", "b2a").then_inc(cond_ready, 1)
                if arg == "2m":
                    plus_bias(10, 2, "bcond2m")
                    modulate("2m", 11, 10, "g2m", "b2m").then_inc(cond_ready, 1)
                if arg == "3":
                    plus_bias(12, 2, "bcond3")
                    link(nc.vector.tensor_scalar(tmp[:, 1, :], cnd[:, 12, :], 1.0, 0.1, ALU.add, ALU.max))
                    for which in ("3a", "3m"):
                        nc.vector.tensor_scalar(mod_a[:, NO[which], :], tmp[:, 1, :], 10.0, vcol("g3"), ALU.min, ALU.mult)
                        last = nc.vector.tensor_copy(mod_b[:, NO[which], :], cnd[:, 13, :])
                    last.then_inc(cond_ready, 1)
                    dve.wait_ge(row_loaded, 32)
                    nc.vector.tensor_scalar(masked[:, :, 0, :], mask_i[:, :, :], 0.0, MASKED, ALU.is_equal, ALU.mult)\
                        .then_inc(mask_ready, 1)

            def dense(step):
                _, u, kind, arg, banks = step
                b = banks[0] if banks else None
                ps = ps_dense[b] if banks else None
                if kind == "cond":
                    condition(step)
                if kind == "enter":
                    nc.vector.memset(v_pad[u][:, :, :, :], 0.0).then_inc(v_cleared, 1)
                if kind == "stats":
                    if arg == "0a":
                        dve.wait_ge(x_loaded, 16)
                    else:
                        wait_filled(dve, step, b)
                    statistics(u, arg, row_source(u, arg))
                if kind == "normed":
                    src = row_source(u, arg)
                    dve.wait_ge(rstd_ready[u], NO[arg] + 1)
                    for s in range(S):
                        if arg[0] == "3":
                            last = nc.vector.tensor_scalar(xhat[u][:, s, :], src(s), rstd[:, u, s:s + 1], None, ALU.mult)
                        else:
                            last = nc.vector.tensor_scalar(xhat[u][:, s, :], src(s), mv[:, u, s, 0:1], rstd[:, u, s:s + 1],
                                                           ALU.subtract, ALU.mult)
                    if arg in ("0a", "1s"):
                        last.then_inc(xhat_ready[u], 1)
                    else:
                        last.then_inc(drained[step_of[u, "stats", arg][4][0]], 1)
                if kind == "v":
                    wait_filled(dve, step, b)
                    if arg == 0:
                        dve.wait_ge(v_cleared, u + 1)
                    for s in range(S):
                        dst = v_pad[u][:, s, :, :].rearrange("p (j i) c -> p j (i c)", i=GH)
                        dst = bass.AP(dst.tensor, dst.offset, [dst.ap[0], [GH * 32, NG], [32 + HD, GH], [1, HD]])
                        last = nc.vector.tensor_copy(dst, ps[:, s * D:(s + 1) * D].rearrange("p (j i d) -> p j i d", j=NG, i=GH))
                    last.then_inc(drained[b], 1)
                if kind == "out" and arg == 0:
                    wait_filled(dve, step, b)
                    for s in range(S):
                        last = nc.vector.scalar_tensor_tensor(xT[u][:, s, :], ps[:, s * T:(s + 1) * T], cnd[:, 2, S * u + s:S * u + s + 1],
                                                              xT[u][:, s, :], ALU.mult, ALU.add)
                    last.then_inc(x_ready[u], 1)
                if (kind == "out" and arg) or (kind == "down" and arg):
                    wait_filled(dve, step, b)
                    bias = {("out", 2): bo2_full[:, :], ("out", 3): vcol("bo3"), ("down", 2): vcol("bdown2"),
                            ("down", 3): vcol("bdown3")}[kind, arg]
                    nc.vector.scalar_tensor_tensor(xT[u][:, :, :], by_seq(ps[:, 0:N]), bias, xT[u][:, :, :], ALU.add, ALU.add)\
                        .then_inc(x_ready[u], 1)
                if kind == "down" and arg == 0:
                    wait_filled(dve, step, b)
                    add_scaled(step, "bdown0", lambda i: cnd[:, 5, i:i + 1])
                if kind == "lin_out":
                    wait_filled(dve, step, b)
                    add_scaled(step, "bo1", lambda i: vec[:, VCOL["c"].start + i:VCOL["c"].start + i + 1])
                if kind == "gated":
                    n = gated_no[step]
                    dve.wait_ge(gate_halves, n + 1)
                    link(nc.vector.scalar_tensor_tensor(silu_g[:, n % 2, :], th[:, n % 2, :], 1.0, half[:, n % 2, :], ALU.add, ALU.mult))
                    nc.vector.scalar_tensor_tensor(hid[u][:, arg, :], ps[:, N:2 * N], vcol("bup3", FC + arg), silu_g[:, n % 2, :],
                                                   ALU.add, ALU.mult).then_inc(drained[b], 1)
                if kind == "lin_qk":
                    wait_filled(dve, step, b)
                    dve.wait_ge(row_loaded, 32)
                    nc.vector.tensor_tensor(l_q[u][:, :, :], by_seq(ps[:, 0:N]), rows[:, 0, :, :].broadcast_to([128, S, D]), ALU.add)
                    nc.vector.tensor_scalar(l_k[u][:, :, :], by_seq(ps[:, N:2 * N]), vcol("bk1"), None, ALU.add).then_inc(drained[b], 1)
                    wait_done(dve, step, b)
                    heads = l_q[u][:, :, :].rearrange("p s (h d) -> p (s h) d", d=HD)
                    nc.vector.tensor_reduce(k_max[:, u, :], l_k[u][:, :, :], AX.X, ALU.max, negate=True)
                    link(nc.vector.tensor_reduce(q_max[:, u, :], heads, AX.X, ALU.max, negate=True))
                    nc.vector.tensor_tensor(l_qs[u][:, :, :].rearrange("p s (h d) -> p (s h) d", d=HD), heads,
                                            q_max[:, u, :].rearrange("p (h o) -> p h o", o=1).broadcast_to([128, S * H, HD]),
                                            ALU.add).then_inc(lin_sub[u], 1)
                if kind == "lin_v":
                    wait_filled(dve, step, b)
                    nc.vector.tensor_tensor(l_v[u][:, :, :], by_seq(ps[:, 0:N]), rows[:, 1, :, :].broadcast_to([128, S, D]), ALU.add)\
                        .then_inc(drained[b], 1)
                if kind == "lin_turn":
                    dve.wait_ge(lin_exp[u], 1)
                    link(nc.vector.tensor_reduce(q_sum[:, u, :], l_e[u][:, 0, :, :].rearrange("p s (h d) -> p (s h) d", d=HD), AX.X, ALU.add))
                    nc.vector.reciprocal(q_inv[:, u, :], q_sum[:, u, :])
                    link(nc.vector.reciprocal(k_inv[:, u, :], k_sum[:, u, :]))
                if kind == "lin_ctx":
                    wait_filled(dve, step, b)
                    for s in range(S):
                        last = nc.vector.scalar_tensor_tensor(l_ctx[u][:, s, :], ps[:, s * D:(s + 1) * D], k_inv[:, u, s:s + 1], blocks,
                                                              ALU.mult, ALU.mult)
                    last.then_inc(drained[b], 1)
                if kind == "lin_y":
                    wait_filled(dve, step, b)
                    nc.vector.tensor_tensor(l_y[u][:, :, :].rearrange("p s (h d) -> p (s h) d", d=HD),
                                            ps[:, 0:N].rearrange("p (h d) -> p h d", d=HD),
                                            q_inv[:, u, :].rearrange("p (h o) -> p h o", o=1).broadcast_to([128, S * H, HD]),
                                            ALU.mult).then_inc(drained[b], 1)
                    wait_done(dve, step, b)
                    statistics(u, "1s", row_source(u, "1s"))
                if kind == "turned" and arg == "1s":
                    dve.wait_ge(lin_tanh[u], 1)
                    nc.vector.scalar_tensor_tensor(l_hs[u][:, :, :], l_t[u][:, :, :], 1.0, hT[u][:, :, :], ALU.add, ALU.mult)\
                        .then_inc(lin_silu[u], 1)

            for t, steps in slots(DVE_LATER):
                if 0 <= t - MAXIMA < NGROUPS:
                    maxima(t - MAXIMA)
                if 0 <= t - TURNED_OUT < NGROUPS:
                    turned_out(t - TURNED_OUT)
                if done(t, INVERSE) is not None:
                    inverse(done(t, INVERSE))
                if done(t, NORMALISE) is not None:
                    normalise(done(t, NORMALISE))
                for step in steps:
                    dense(step)

        @block.tensor
        def _(pe):
            def scores(g):
                layer, u, s, j = group(g)
                if j == 0 and s == 0:
                    pe.wait_ge(stacked[u % 2], STACKING * ((U * att_no(layer) + u) // 2 + 1))
                if g >= NSC:
                    pe.wait_ge(probs_ready, g - NSC + 1)
                ps = ps_scores[g % NSC]
                last = nc.tensor.matmul(ps[:, :], q_stack[u][:, j, s * T:(s + 1) * T], k_stack[u][:, j, :, s * T:(s + 1) * T],
                                        start=True, stop=True)
                last.then_inc(scores_ready, 1)

            def turn(g):
                pe.wait_ge(probs_ready, g + 1)
                if g >= NTU:
                    pe.wait_ge(turned_read, g - NTU + 1)
                for i in range(GH):
                    last = nc.tensor.transpose(ps_turned[g % NTU][:, i * T:(i + 1) * T], probs[:, g % 4, i, :], ident)
                last.then_inc(turned_ready, 1)

            def values(q):
                layer, u, s, _ = group(q * NG)
                pe.wait_ge(turned_read, NG * (q + 1))
                wait_written(pe, u, "v", layer)
                if q >= 1:
                    pe.wait_ge(att_read, q)
                for i in range(GH):
                    for j in range(NG):
                        h = GH * j + i
                        nc.tensor.matmul(ps_att[32 * j:32 * j + 32, 0:T], v_pad[u][:, s, h, :], probsT[:, q % 2, h, :],
                                         start=i == 0, stop=i == GH - 1)
                pe.wait_ge(rden_ready, q + 1)
                nc.tensor.transpose(ps_att[:, T:2 * T], rden_wide[:, q % 2, :, :].rearrange("p h d -> p (h d)"), ident)\
                    .then_inc(att_ready, 1)

            def dense(step):
                _, u, kind, arg, banks = step
                for b in banks:
                    wait_free(pe, step, b)
                b = banks[0] if banks else None
                ps = ps_dense[b] if banks else None
                flat = lambda tile: tile.rearrange("p s t -> p (s t)")
                h_flat = flat(hT[u][:, :, :])

                def mm(out, lhsT, rhs, start=True, stop=True):
                    return nc.tensor.matmul(out, lhsT, rhs, start=start, stop=stop)

                if kind == "cond":
                    pe.wait_ge(silu_ready, 1)
                    name = f"cond{arg}"
                    wait_weights(pe, name)
                    rhs = vec[:, VCOL["c"]] if arg[0] == "2" else sil[:, :]
                    for i in range(6 if arg == "0" else 2):
                        last = mm(ps[:, i * B:(i + 1) * B], wcol(name, i), rhs)
                    if arg == "2a":
                        last = mm(ps[:, 2 * B:2 * B + 1], wcol("o2"), vcol("bv2"))
                    last.then_inc(filled[b], 1)
                if kind == "enter":
                    pe.wait_ge(x_loaded, 16)
                    pe.wait_ge(const_loaded, 16)
                    for s in range(S):
                        last = nc.tensor.transpose(ps[:, s * T:(s + 1) * T], x_tok[:, S * u + s, :], ident)
                    last.then_inc(filled[b], 1)
                if kind == "stats" and banks:
                    pe.wait_ge(x_ready[u], BEFORE_NORM[arg])
                    for s in range(S):
                        last = nc.tensor.transpose(ps[:, s * T:(s + 1) * T], xT[u][:, s, :], ident)
                    last.then_inc(filled[b], 1)
                if kind == "turned":
                    if arg in ("0a", "1s"):
                        pe.wait_ge(xhat_ready[u], 1 if arg == "0a" else 2)
                    else:
                        wait_written(pe, u, "stats", arg)
                    for s in range(S):
                        last = nc.tensor.transpose(ps[:, s * T:(s + 1) * T], xhat[u][:, s, :], ident)
                    last.then_inc(filled[b], 1)
                if kind == "qk":
                    wait_written(pe, u, "turned", f"{arg}a")
                    wait_weights(pe, f"q{arg}")
                    mm(ps[:, 0:N], wcol(f"q{arg}"), h_flat)
                    mm(ps[:, N:2 * N], wcol(f"k{arg}"), h_flat).then_inc(filled[b], 1)
                if kind in ("v", "lin_v"):
                    for s in range(S):
                        last = mm(ps[:, s * D:(s + 1) * D], hT[u][:, s, :], wcol(f"v{arg}"))
                    last.then_inc(filled[b], 1)
                if kind == "out":
                    pe.wait_ge(att_read, B * att_no(arg) + S * (u + 1))
                    wait_weights(pe, f"o{arg}")
                    mm(ps[:, 0:N], wcol(f"o{arg}"), flat(att[u][:, :, :])).then_inc(filled[b], 1)
                if kind == "up":
                    wait_written(pe, u, "turned", f"{arg}m")
                    wait_weights(pe, f"up{arg}")
                    for c in range(FC):
                        last = mm(ps_dense[banks[c // 2]][:, (c % 2) * N:(c % 2 + 1) * N], wcol(f"up{arg}", c), h_flat)
                        if c % 2:
                            last.then_inc(filled[banks[c // 2]], 1)
                if kind == "gated":
                    wait_written(pe, u, "turned", "3m")
                    wait_weights(pe, "up3")
                    mm(ps[:, 0:N], wcol("up3", arg), h_flat)
                    mm(ps[:, N:2 * N], wcol("up3", FC + arg), h_flat).then_inc(filled[b], 1)
                if kind == "down":
                    if arg == 3:
                        for c in range(FC):
                            wait_written(pe, u, "gated", c)
                    else:
                        wait_written(pe, u, "up", arg)
                    for c in range(FC):
                        last = mm(ps[:, 0:N], wcol(f"down{arg}", c), hid[u][:, c, :], start=c == 0, stop=c == FC - 1)
                    last.then_inc(filled[b], 1)
                if kind == "lin_qk":
                    wait_written(pe, u, "turned", "1a")
                    wait_weights(pe, "q1")
                    for s in range(S):
                        mm(ps[:, s * D:(s + 1) * D], hT[u][:, s, :], wcol("q1"))
                    mm(ps[:, N:2 * N], wcol("k1"), h_flat).then_inc(filled[b], 1)
                if kind == "lin_turn":
                    pe.wait_ge(lin_exp[u], 1)
                    for i in range(2 * S):
                        last = nc.tensor.transpose(ps[:, i * T:(i + 1) * T], l_e[u][:, i // S, i % S, :], ident)
                    last.then_inc(filled[b], 1)
                if kind == "lin_ctx":
                    wait_written(pe, u, "lin_turn", 1)
                    wait_written(pe, u, "lin_v", 1)
                    for s in range(S):
                        last = mm(ps[:, s * D:(s + 1) * D], l_eT[u][:, (S + s) * T:(S + s + 1) * T], l_v[u][:, s, :])
                    last.then_inc(filled[b], 1)
                if kind == "lin_y":
                    wait_written(pe, u, "lin_ctx", 1)
                    for s in range(S):
                        last = mm(ps[:, s * D:(s + 1) * D], l_eT[u][:, s * T:(s + 1) * T], l_ctx[u][:, s, :])
                    last.then_inc(filled[b], 1)
                if kind == "lin_out":
                    pe.wait_ge(lin_silu[u], 1)
                    mm(ps[:, 0:N], wcol("o1"), flat(l_hs[u][:, :, :])).then_inc(filled[b], 1)
                if kind == "leave":
                    pe.wait_ge(x_ready[u], len(SUMS))
                    for s in range(S):
                        last = nc.tensor.transpose(ps[:, s * T:(s + 1) * T], xT[u][:, s, :], ident)
                    last.then_inc(filled[b], 1)

            for t, steps in slots():
                if 0 <= t - SCORES < NGROUPS:
                    scores(t - SCORES)
                if 0 <= t - TURN < NGROUPS:
                    turn(t - TURN)
                if done(t, VALUES) is not None:
                    values(done(t, VALUES))
                for step in steps:
                    dense(step)


def kernel(**inputs):
    import numpy as np
    import concourse.bacc as bacc
    from concourse.bass_utils import run_bass_kernel_spmd

    def arr(name):
        return np.asarray(inputs[name])

    def cols(name):
        return arr(name).reshape(-1, 128).T

    def chunked(m):
        return m.reshape(-1, 128, m.shape[1]).transpose(1, 0, 2).reshape(128, -1)

    def per_query_head(m):
        return np.repeat(m.reshape(HD // 2, HD, D), GH, axis=0).reshape(D, D)

    qkv3 = arr("L3_cond_qkv_w")
    weights = {
        "cond0": arr("L0_cond_wc").T, "q0": arr("L0_cond_wq").T, "k0": per_query_head(arr("L0_cond_wk")).T,
        "v0": per_query_head(arr("L0_cond_wv")).T, "o0": arr("L0_cond_wo").T, "up0": arr("L0_cond_w1").T,
        "down0": chunked(arr("L0_cond_w2").T),
        "cond1": arr("L1_cond_emb_W"), "q1": arr("L1_cond_Wq"), "k1": arr("L1_cond_Wk"), "v1": arr("L1_cond_Wv"),
        "o1": arr("L1_cond_out_W"),
        "cond2a": arr("L2_cond_wt_attn"), "cond2m": arr("L2_cond_wt_ffn"), "q2": arr("L2_cond_wq"), "k2": arr("L2_cond_wk"),
        "v2": arr("L2_cond_wv"), "o2": arr("L2_cond_wo"), "up2": arr("L2_cond_w1"), "down2": chunked(arr("L2_cond_w2")),
        "cond3": np.concatenate([arr("L3_cond_scale_w").T, arr("L3_cond_shift_w").T], axis=1),
        "q3": qkv3[0:D].T, "k3": qkv3[D:2 * D].T, "v3": qkv3[2 * D:].T, "o3": arr("L3_cond_proj_w").T,
        "up3": arr("L3_cond_mlp_w1").T, "down3": chunked(arr("L3_cond_mlp_w2").T),
    }
    vectors = {
        "c": arr("cond_1024").T, "bc0": cols("L0_cond_bc"), "bup0": cols("L0_cond_b1"), "bdown0": cols("L0_cond_b2"),
        "g1": cols("L1_cond_norm_g"), "b1": cols("L1_cond_norm_b"), "bk1": cols("L1_cond_bk"), "bcond1": cols("L1_cond_emb_b"),
        "gs1": cols("L1_cond_sn_g"), "bs1": cols("L1_cond_sn_b"), "bo1": cols("L1_cond_out_b"),
        "g2a": cols("L2_cond_ln1_w"), "b2a": cols("L2_cond_ln1_b"), "g2m": cols("L2_cond_ln2_w"), "b2m": cols("L2_cond_ln2_b"),
        "bq2": cols("L2_cond_bq"), "bk2": cols("L2_cond_bk"), "bv2": cols("L2_cond_bv"), "bo2": cols("L2_cond_bo"),
        "bcond2a": cols("L2_cond_bt_attn"), "bcond2m": cols("L2_cond_bt_ffn"), "bup2": cols("L2_cond_b1"),
        "bdown2": cols("L2_cond_b2"), "g3": cols("L3_cond_norm_w"),
        "bcond3": np.concatenate([cols("L3_cond_scale_b"), cols("L3_cond_shift_b")], axis=1),
        "bo3": cols("L3_cond_proj_b"), "bup3": cols("L3_cond_mlp_b1"), "bdown3": cols("L3_cond_mlp_b2"),
    }
    head = np.arange(D) // HD
    const = np.concatenate([
        np.eye(D), head[:, None] == head[None, :], np.full((D, S), -0.5),
    ], axis=1).astype(np.float32)
    arrays = {
        "x": np.ascontiguousarray(arr("x")),
        "vectors": np.ascontiguousarray(np.concatenate([vectors[n] for n, _ in VECTORS], axis=1)),
        "weights": np.ascontiguousarray(np.concatenate([weights[n] for n, _ in WEIGHTS], axis=1)),
        "row_biases": np.concatenate([arr("L1_cond_bq"), arr("L1_cond_bv")]),
        "mask": np.ascontiguousarray(arr("mask_BxS_ik0")).reshape(-1),
        "constants": const,
        "pads": np.stack([np.repeat(np.arange(D)[:, None] % HD == 0, N, axis=1), np.zeros((D, N))]).astype(np.float32),
    }
    nc = bacc.Bacc("TRN2", target_bir_lowering=False, num_devices=1)
    args = [nc.dram_tensor(n, a.shape, mybir.dt.from_np(a.dtype), kind="ExternalInput").ap() for n, a in arrays.items()]
    out = nc.dram_tensor("out", (B, T, D), F32, kind="ExternalOutput").ap()
    parts = nc.dram_tensor("parts", (2, 2, D, ROWS, N), F32, kind="Internal").ap()
    build(nc, *args, parts, out)
    r = run_bass_kernel_spmd(nc, [arrays], core_ids=[0])
    return r.results[0]["out"]
```

```python
from contextlib import ExitStack

import concourse.bass as bass
from concourse import mybir

F32 = mybir.dt.float32
F32R = mybir.dt.float32r
I32 = mybir.dt.int32
ALU = mybir.AluOpType
ACT = mybir.ActivationFunctionType
AX = mybir.AxisListType

B, T, D = 8, 128, 128
H, HD = 16, 8
GH = 4
NG = H // GH
U = 4
S = B // U
N = S * T
F = 512
FC = F // D
NATT = 3
NGROUPS = NATT * B * NG
NSEQ = NATT * B
NSC, NTU, NDENSE = 3, 1, 3
TERMS = 3
ROWS = 4
PARTS = 16 * 4
STACKING = 16 * (1 + GH)
MASKED = -2.0 ** 100

WEIGHTS = [
    ("cond0", 6 * D), ("q0", D), ("k0", D), ("v0", D), ("o0", D), ("up0", F), ("down0", F),
    ("cond1", 2 * D), ("q1", D), ("k1", D), ("v1", D), ("o1", D),
    ("cond2a", 2 * D), ("cond2m", 2 * D), ("q2", D), ("k2", D), ("v2", D), ("o2", D), ("up2", F), ("down2", F),
    ("cond3", 2 * D), ("q3", D), ("k3", D), ("v3", D), ("o3", D), ("up3", 2 * F), ("down3", F),
]
LOADS = [("cond0",), ("q0", "k0", "v0"), ("o0", "up0", "down0"), ("cond1", "q1", "k1", "v1", "o1"),
         ("cond2a", "cond2m", "q2", "k2", "v2", "o2"), ("up2", "down2"), ("cond3", "q3", "k3", "v3", "o3"),
         ("up3", "down3")]
VECTORS = [
    ("c", B), ("bc0", 6), ("bup0", FC), ("bdown0", 1),
    ("g1", 1), ("b1", 1), ("bk1", 1), ("bcond1", 2), ("gs1", 1), ("bs1", 1), ("bo1", 1),
    ("g2a", 1), ("b2a", 1), ("g2m", 1), ("b2m", 1), ("bq2", 1), ("bk2", 1), ("bv2", 1), ("bo2", 1),
    ("bcond2a", 2), ("bcond2m", 2), ("bup2", FC), ("bdown2", 1),
    ("g3", 1), ("bcond3", 2), ("bo3", 1), ("bup3", 2 * FC), ("bdown3", 1),
]
CONST = 2 * D + S
NORMS = ["0a", "0m", "1a", "1s", "2a", "2m", "3a", "3m"]
EPS = 1e-5
EPS3 = 1e-6


def columns(items):
    at, out = 0, {}
    for name, n in items:
        out[name] = slice(at, at + n)
        at += n
    return out, at


WCOL, WTOTAL = columns(WEIGHTS)
VCOL, VTOTAL = columns(VECTORS)


def norm_steps(which):
    return [("stats", which), ("normed", which), ("turned", which)]


PHASES = [
    [("enter", 0), *norm_steps("0a"), ("qk", 0), ("v", 0)],
    [("out", 0), *norm_steps("0m"), ("up", 0), ("down", 0), *norm_steps("1a"), ("lin_qk", 1), ("lin_v", 1), ("lin_turn", 1),
     ("lin_ctx", 1), ("lin_y", 1), ("normed", "1s"), ("turned", "1s"), ("lin_out", 1), *norm_steps("2a"), ("qk", 2), ("v", 2)],
    [("out", 2), *norm_steps("2m"), ("up", 2), ("down", 2), *norm_steps("3a"), ("qk", 3), ("v", 3)],
    [("out", 3), *norm_steps("3m"), *[("gated", c) for c in range(FC)], ("down", 3), ("leave", 3)],
]
AFTER = {
    ("normed", "0a"): [("pool", "stats", "0a")], ("turned", "0a"): [("dve", "normed", "0a")],
    ("qk", 0): [("act", "turned", "0a")], ("v", 0): [("act", "turned", "0a"), ("dve", "enter", 0)],
    ("stats", "0m"): [("dve", "out", 0)], ("up", 0): [("act", "turned", "0m")], ("down", 0): [("act", "up", 0)],
    ("stats", "1a"): [("dve", "down", 0)],
    ("lin_qk", 1): [("act", "turned", "1a")], ("lin_v", 1): [("act", "turned", "1a")], ("lin_turn", 1): [("act", "lin_qk", 1)],
    ("lin_ctx", 1): [("act", "lin_turn", 1), ("dve", "lin_turn", 1), ("dve", "lin_v", 1)], ("lin_y", 1): [("dve", "lin_ctx", 1)],
    ("normed", "1s"): [("pool", "lin_y", 1)], ("lin_out", 1): [("dve", "turned", "1s")],
    ("stats", "2a"): [("dve", "lin_out", 1)], ("qk", 2): [("act", "turned", "2a")], ("v", 2): [("act", "turned", "2a")],
    ("stats", "2m"): [("dve", "out", 2)], ("up", 2): [("act", "turned", "2m")], ("down", 2): [("act", "up", 2)],
    ("stats", "3a"): [("dve", "down", 2)], ("qk", 3): [("act", "turned", "3a")], ("v", 3): [("act", "turned", "3a")],
    ("stats", "3m"): [("dve", "out", 3)],
    **{("gated", c): [("act", "turned", "3m")] for c in range(FC)},
    ("down", 3): [("dve", "gated", c) for c in range(FC)], ("leave", 3): [("dve", "down", 3)],
    **{("normed", n): [("pool", "stats", n)] for n in ("0m", "1a", "2a", "2m", "3a", "3m")},
    **{("turned", n): [("dve", "normed", n)] for n in ("0m", "1a", "1s", "2a", "2m", "3a", "3m")},
}
PARTS_OF = {
    "cond": [("pe", 0.4), ("dve", 0.6)], "enter": [("pe", 0.22), ("act", 0.26)],
    "stats": [("pe", 0.22), ("dve", 0.9), ("pool", 0.63)], "normed": [("dve", 0.52)],
    "turned": [("pe", 0.22), ("act", 0.68)], "qk": [("pe", 0.86), ("act", 0.52), ("pool", 3.2), ("sp", 8.0)],
    "v": [("pe", 0.43), ("dve", 0.4)], "out": [("pe", 0.43), ("dve", 0.4)], "up": [("pe", 1.72), ("act", 3.9)],
    "down": [("pe", 1.72), ("dve", 0.4)], "lin_qk": [("pe", 0.86), ("dve", 1.9), ("act", 1.0)],
    "lin_v": [("pe", 0.43), ("dve", 0.33)], "lin_turn": [("pe", 0.44), ("act", 0.46)], "lin_ctx": [("pe", 0.43), ("dve", 0.5)],
    "lin_y": [("pe", 0.43), ("dve", 1.3), ("pool", 0.63)], "lin_out": [("pe", 0.43), ("dve", 1.1)],
    "gated": [("pe", 0.86), ("act", 0.52), ("dve", 0.7)], "leave": [("pe", 0.22), ("act", 0.26), ("sp", 2.0)],
}
LAST_READER = {"enter": "act", "turned": "act", "qk": "act", "up": "act", "lin_turn": "act", "leave": "act"}
MOMENT = 0.1
HAND_OVER = 0.15
START = [-12, -11, -2, 5]
FIRSTS = [0, 1, 1, 1]
SPACING = [1, 0.6, 0.8, 0.8]
CONDITIONS = [("0", -9.5), ("1", 1.1), ("2a", 2.1), ("2m", 3.1), ("3", 4.1)]
RANKS = {"scores": -1, "maxima": -1, "exps": 0, "turn": 0, "turned_out": 0, "inverse": 0, "values": 0, "inverse_sums": 0,
         "normalise": 0}


def plan():
    parts = {}

    def add(name, cost, after, rank):
        parts[name] = (name[0], cost, [n for n in after if n in parts or n is not None], rank)

    def add_step(u, kind, arg, rank, first_after):
        previous = first_after
        for engine, cost in PARTS_OF[kind]:
            if (kind, arg, engine) == ("stats", "0a", "pe"):
                continue
            if kind == "cond" and arg == "0" and engine == "pe":
                cost = 2.6
            add((engine, u, kind, arg), cost, previous, rank)
            previous = [(engine, u, kind, arg)]

    for i, (name, rank) in enumerate(CONDITIONS):
        add_step(0, "cond", name, rank, [("dve", 0, "cond", CONDITIONS[i - 1][0])] if i else [])
    for u in range(U):
        for phase, kinds in enumerate(PHASES):
            end = S * NG * (u + 1) + B * NG * (phase - 1)
            rank = START[u] if phase == 0 else end + FIRSTS[phase]
            for kind, arg in kinds:
                after = [(e, u, k, a) for e, k, a in AFTER.get((kind, arg), [])]
                if kind == "out":
                    after.append(("dve", "normalise", end // NG - 1))
                if kind in ("enter", "leave", "qk", "gated") and u:
                    for engine, _ in PARTS_OF[kind]:
                        after.append((engine, u - 1, kind, arg if kind != "gated" else FC - 1))
                if kind == "gated" and arg:
                    after.append(("dve", u, kind, arg - 2) if arg > 1 else ("pe", u, kind, 0))
                    after.append(("act", u, kind, arg - 1))
                if kind == "qk" and arg and not u:
                    after.append(("sp", U - 1, "qk", 0 if arg == 2 else 2))
                if u >= 2 and kind in ("up", "lin_qk"):
                    after.append(("dve", u - 2, "down" if kind == "up" else "lin_out", arg))
                add_step(u, kind, arg, rank, after)
                if kind == "enter":
                    add(("dve", u, kind, arg), 1.07, [("dve", u - 1, kind, arg)] if u else [], rank)
                if kind == "lin_turn":
                    add(("dve", u, kind, arg), 0.6, [("act", u, "lin_qk", 1)], rank)
                if (kind, arg) == ("turned", "1s"):
                    add(("dve", u, kind, arg), 0.35, [("act", u, kind, arg)], rank)
                if kind == "turned":
                    cond = {"0": "0", "1": "1", "2": "2m", "3": "3"}[arg[0]]
                    parts["act", u, kind, arg][2].append(("dve", 0, "cond", cond))
                rank += SPACING[phase]

    for g in range(NGROUPS):
        q, j = divmod(g, NG)
        a, r = divmod(q, B)
        u = r // S

        def step(what, engine, cost, which, after):
            before_it = [(engine, what, which - 1)] if which else []
            add((engine, what, which), cost, before_it + [n for n, ok in after if ok], g + RANKS[what])

        step("scores", "pe", 0.22, g, [(("sp", u, "qk", (0, 2, 3)[a]), True), (("act", "exps", g - NSC), g >= NSC)])
        step("maxima", "dve", 0.6, g, [(("pe", "scores", g), True)])
        step("exps", "act", 1.37, g, [(("dve", "maxima", g), True), (("pe", "turn", g - 4), g >= 4)])
        step("turn", "pe", 0.44, g, [(("act", "exps", g), True), (("dve", "turned_out", g - NTU), g >= NTU)])
        step("turned_out", "dve", 0.6, g, [(("pe", "turn", g), True), (("pe", "values", q - 2), q >= 2)])
        if j == NG - 1:
            step("inverse", "dve", 0.3, q, [(("act", "exps", g), True), (("pe", "values", q - 2), q >= 2)])
            step("values", "pe", 1.4, q, [(("dve", "turned_out", g), True), (("dve", "inverse", q), True),
                                          (("dve", u, "v", (0, 2, 3)[a]), True), (("dve", "normalise", q - 1), q >= 1)])
            step("inverse_sums", "act", 0.25, q, [(("pe", "values", q), True)])
            step("normalise", "dve", 0.25, q, [(("act", "inverse_sums", q), True)])

    waiting = {n: len(set(p[2])) for n, p in parts.items()}
    followers = {n: [] for n in parts}
    for n, p in parts.items():
        for m in set(p[2]):
            followers[m].append(n)
    ready = {n for n, k in waiting.items() if not k}
    over = {}
    free_at = {"pe": 6.6, "act": 6.6, "dve": 7.0, "pool": 6.0, "sp": 0.0}
    bank_free = {b: 0.0 for b in range(NDENSE)}
    banks_of, order, steps = {}, {e: [] for e in free_at}, []

    def banks_for(name):
        if name[0] != "pe" or len(name) != 4:
            return 0
        return 2 if name[2] == "up" else 1

    while ready:
        best = None
        for n in ready:
            engine, cost, after, rank = parts[n]
            start = max([free_at[engine]] + [over[m] + (HAND_OVER if m[0] != engine else 0) for m in after])
            k = banks_for(n)
            if k:
                if len(bank_free) < k:
                    continue
                start = max(start, sorted(bank_free.values())[k - 1] + HAND_OVER)
            free_of = max(start, free_at[engine])
            if best is None or (free_of, rank, n[1:] and str(n)) < best[:3]:
                best = (free_of, rank, str(n), n)
        earliest, _, _, first = best
        engine = first[0]
        choice = None
        for n in ready:
            if n[0] != engine:
                continue
            _, cost, after, rank = parts[n]
            start = max([free_at[engine]] + [over[m] + (HAND_OVER if m[0] != engine else 0) for m in after])
            k = banks_for(n)
            if k:
                if len(bank_free) < k:
                    continue
                start = max(start, sorted(bank_free.values())[k - 1] + HAND_OVER)
            if start <= earliest + MOMENT and (choice is None or (rank, str(n)) < choice[:2]):
                choice = (rank, str(n), n, start)
        _, _, name, start = choice
        cost = parts[name][1]
        over[name] = start + cost
        free_at[engine] = start + (4.5 if name[0] == "sp" else cost)
        ready.remove(name)
        order[engine].append(name)
        for m in followers[name]:
            waiting[m] -= 1
            if not waiting[m]:
                ready.add(m)
        if len(name) == 4:
            _, u, kind, arg = name
            k = banks_for(name)
            if k:
                took = tuple(sorted(bank_free, key=lambda b: (bank_free[b], b))[:k])
                for b in took:
                    del bank_free[b]
                banks_of[u, kind, arg] = took
                steps.append((u, kind, arg, took))
            elif name[0] == "dve" and (kind == "normed" or (kind, arg) == ("stats", "0a")):
                steps.append((u, kind, arg, ()))
            if kind == "normed" and (u, "stats", arg) in banks_of:
                bank_free.update({b: over[name] for b in banks_of[u, "stats", arg]})
            elif kind not in ("stats", "normed") and name[0] == LAST_READER.get(kind, "dve"):
                bank_free.update({b: over[name] for b in banks_of[u, kind, arg]})
    assert len(over) == len(parts)
    by_name = {s[:3]: (None, *s) for s in steps}
    return [(None, *s) for s in steps], {
        e: [(n[1], n[2]) if len(n) == 3 else ("dense", by_name[n[1:]]) for n in names] for e, names in order.items()}


def build(nc, x_in, c_in, w_in, rows_in, mask_in, const_in, pads_in, parts, out):
    with ExitStack() as ctx:
        def sb(name, shape, dt=F32):
            return ctx.enter_context(nc.sbuf_tensor(name, shape, dt))

        def sem(name):
            return ctx.enter_context(nc.semaphore(name))

        def sems(name, n):
            return [sem(f"{name}{i}") for i in range(n)]

        w = sb("w", [128, WTOTAL])
        vec = sb("vec", [128, VTOTAL])
        rows = sb("rows", [128, 2, 1, D])
        mask_i = sb("mask_i", [128, B, T], I32)
        masked = sb("masked", [128, B, 1, T], F32R)
        const = sb("const", [128, CONST])
        ident = const[:, 0:D]
        blocks = const[:, D:2 * D]
        minus_half = const[:, 2 * D:CONST]

        x_tok = sb("x_tok", [128, B, D])
        y_tok = sb("y_tok", [128, B, D])

        def per_unit(name, shape, n=U, dt=F32):
            tiles = [sb(f"{name}{i}", shape, dt) for i in range(n)]
            return [tiles[u % n] for u in range(U)]

        xT = per_unit("xT", [128, S, T])
        xhat = per_unit("xhat", [128, S, D])
        hT = per_unit("hT", [128, S, T])
        qkT = per_unit("qkT", [128, 2, S, T], 2)
        qk_high = per_unit("qk_high", [128, 2, N], 2, F32R)
        qk_low = per_unit("qk_low", [128, 2, N], 2, F32R)
        q_stack = per_unit("q_stack", [128, NG, N], 2, F32R)
        k_stack = per_unit("k_stack", [128, NG, GH, N], 2, F32R)
        v_pad = per_unit("v_pad", [128, S, H, 32])
        att = per_unit("att", [128, S, T])
        scaled = per_unit("scaled", [128, S, T], 2)
        hid = per_unit("hid", [128, FC, N], 2)
        th = sb("th", [128, 2, N])
        half = sb("half", [128, 2, N])
        silu_g = sb("silu_g", [128, 2, N])
        bn = sb("bn", [128, U, S, 6])
        mv = sb("mv", [128, U, S, 2])
        base = sb("base", [128, U, S])
        rstd = sb("rstd", [128, U, S])
        l_q = per_unit("l_q", [128, S, D], 2)
        l_qs = per_unit("l_qs", [128, S, D], 2)
        l_k = per_unit("l_k", [128, S, T], 2)
        l_v = per_unit("l_v", [128, S, D], 2)
        l_e = per_unit("l_e", [128, 2, S, T], 2)
        l_eT = per_unit("l_eT", [128, 2 * S * T], 2)
        l_ctx = per_unit("l_ctx", [128, S, D], 2)
        l_y = per_unit("l_y", [128, S, D], 2)
        l_t = per_unit("l_t", [128, S, T], 2)
        l_hs = per_unit("l_hs", [128, S, T], 2)
        q_max = sb("q_max", [128, U, S * H])
        q_sum = sb("q_sum", [128, U, S * H])
        q_inv = sb("q_inv", [128, U, S * H])
        k_max = sb("k_max", [128, U, S])
        k_sum = sb("k_sum", [128, U, S])
        k_inv = sb("k_inv", [128, U, S])
        c_tanh = sb("c_tanh", [128, B])
        c_half = sb("c_half", [128, B])
        sil = sb("sil", [128, B])
        cnd = sb("cnd", [128, 14, B])
        tmp = sb("tmp", [128, 2, B])
        mod_a = sb("mod_a", [128, len(NORMS), B])
        mod_b = sb("mod_b", [128, len(NORMS), B])
        bq2_scaled = sb("bq2_scaled", [128, 1])
        bo2_full = sb("bo2_full", [128, 1])
        bup3_half = sb("bup3_half", [128, FC])
        probs = sb("probs", [128, 4, GH, T])
        probsT = sb("probsT", [128, 2, H, T])
        neg_max = sb("neg_max", [128, NGROUPS, GH])
        den = sb("den", [128, NSEQ, H])
        rden = sb("rden", [128, NSEQ, H, 1])
        rden_wide = sb("rden_wide", [128, 2, H, HD])
        rdenT = sb("rdenT", [128, 2, T])

        psum = [ctx.enter_context(nc.psum_tensor(f"ps{i}", [128, 512], F32)) for i in range(8)]
        ps_scores, ps_turned, ps_att, ps_dense = psum[0:NSC], psum[NSC:NSC + NTU], psum[7 - NDENSE], psum[8 - NDENSE:]

        x_loaded, vec_loaded, const_loaded, row_loaded = sem("x_loaded"), sem("vec_loaded"), sem("const_loaded"), sem("row_loaded")
        w_loaded = sems("w_loaded", len(LOADS))
        stored = sem("stored")
        c_tanh_ready, silu_ready = sem("c_tanh_ready"), sem("silu_ready")
        cond_ready = sem("cond_ready")
        filled = sems("filled", NDENSE)
        drained = sems("drained", NDENSE)
        x_ready = sems("x_ready", U)
        var_ready, rstd_ready, xhat_ready = sems("var_ready", U), sems("rstd_ready", U), sems("xhat_ready", U)
        split_high, split_low = sem("split_high"), sem("split_low")
        parts_stored, stacked = sems("parts_stored", 2), sems("stacked", 2)
        mask_ready = sem("mask_ready")
        v_cleared = sem("v_cleared")
        stack_cleared = sem("stack_cleared")
        pads_stored = sem("pads_stored")
        lin_sub, lin_exp = sems("lin_sub", U), sems("lin_exp", U)
        lin_tanh, lin_silu = sems("lin_tanh", U), sems("lin_silu", U)
        gate_halves = sem("gate_halves")
        y_ready = sem("y_ready")
        scores_ready, max_ready, probs_ready = sem("scores_ready"), sem("max_ready"), sem("probs_ready")
        turned_ready, turned_read = sem("turned_ready"), sem("turned_read")
        rden_ready, att_ready, rdenT_ready, att_read = sem("rden_ready"), sem("att_ready"), sem("rdenT_ready"), sem("att_read")
        dve_own = sem("dve_own")

        STEPS, ORDER = plan()
        step_of = {(s[1], s[2], s[3]): s for s in STEPS}
        before, fills, drains, last_of = {}, {}, {}, {}
        n_fill, n_drain = [0] * NDENSE, [0] * NDENSE
        SUMS = [("enter", 0), ("out", 0), ("down", 0), ("lin_out", 1), ("out", 2), ("down", 2), ("out", 3), ("down", 3)]
        BEFORE_NORM = {"0m": 2, "1a": 3, "2a": 4, "2m": 5, "3a": 6, "3m": 7}
        for s in STEPS:
            for b in s[4]:
                before[s, b] = last_of.get(b)
                last_of[b] = s
                n_fill[b] += 1
                fills[s, b] = n_fill[b]
                if (s[2], s[3]) not in SUMS and s[2] != "leave":
                    n_drain[b] += 1
                    drains[s, b] = n_drain[b]
        gated_no = {s: i for i, s in enumerate(x for x in STEPS if x[2] == "gated")}

        def wait_done(eng, step, b):
            _, u, kind, arg, _ = step
            if (kind, arg) in SUMS:
                eng.wait_ge(x_ready[u], SUMS.index((kind, arg)) + 1)
            elif kind == "leave":
                eng.wait_ge(y_ready, u + 1)
            else:
                eng.wait_ge(drained[b], drains[step, b])

        def wait_written(eng, u, kind, arg):
            step = step_of[u, kind, arg]
            for b in step[4]:
                wait_done(eng, step, b)

        def wait_free(eng, step, b):
            if before[step, b] is not None:
                wait_done(eng, before[step, b], b)

        def wait_filled(eng, step, b):
            eng.wait_ge(filled[b], fills[step, b])

        def wait_weights(eng, name):
            eng.wait_ge(w_loaded[next(i for i, names in enumerate(LOADS) if name in names)], 16)

        def vcol(name, i=0):
            at = VCOL[name].start + i
            return vec[:, at:at + 1]

        def wcol(name, i=0):
            at = WCOL[name].start + i * D
            return w[:, at:at + D]

        def att_no(layer):
            return (0, 2, 3).index(layer)

        def group(g):
            a, r = divmod(g, B * NG)
            u, r = divmod(r, S * NG)
            return (0, 2, 3)[a], u, r // NG, r % NG

        def by_seq(tile):
            return tile.rearrange("p (s t) -> p s t", s=S)

        NO = {n: i for i, n in enumerate(NORMS)}
        block = ctx.enter_context(nc.Block())

        @block.sync
        def _(sp):
            sp.dma_start(vec[:, :], c_in).then_inc(vec_loaded, 16)
            sp.dma_start(x_tok[:, :, :], x_in.rearrange("b t d -> t b d")).then_inc(x_loaded, 16)
            for i in range(1, len(LOADS), 2):
                cols = slice(WCOL[LOADS[i][0]].start, WCOL[LOADS[i][-1]].stop)
                sp.dma_start(w[:, cols], w_in[:, cols]).then_inc(w_loaded[i], 16)
                if i == 1:
                    for ring in range(2):
                        sp.dma_start(parts[ring, :, :, TERMS, :], pads_in).then_inc(pads_stored, 16)
            sp.wait_ge(pads_stored, 16 * 2)

            def stack(u, layer):
                n = U * att_no(layer) + u
                scratch = parts[n % 2]
                high, low = qk_high[u][:, :, :].bitcast(F32), qk_low[u][:, :, :].bitcast(F32)
                if n >= 2:
                    sp.wait_ge(stacked[n % 2], STACKING * (n // 2))
                sp.wait_ge(split_high, n + 1)
                for a, terms in ((0, slice(0, 2)), (1, slice(0, 3, 2))):
                    sp.dma_start(scratch[a, :, terms, :], high[:, a:a + 1, :].broadcast_to([128, 2, N])).then_inc(parts_stored[n % 2], 16)
                if layer == 3:
                    sp.wait_ge(mask_ready, 1)
                    sp.dma_start(scratch[1].rearrange("(h d) t n -> h d t n", d=HD)[:, 0, TERMS, :],
                                 masked[0:H, S * u:S * (u + 1), 0, :].rearrange("p s t -> p (s t)").bitcast(F32))\
                        .then_inc(parts_stored[n % 2], 16)
                sp.wait_ge(split_low, n + 1)
                for a, t in ((0, 2), (1, 1)):
                    sp.dma_start(scratch[a, :, t, :], low[:, a, :]).then_inc(parts_stored[n % 2], 16)
                if n < 2:
                    sp.wait_ge(stack_cleared, n + 1)
                else:
                    sp.wait_ge(scores_ready, S * NG * (n - 1))
                sp.wait_ge(parts_stored[n % 2], PARTS * (n // 2 + 1) + 16 * (layer == 3) * (u // 2 + 1))
                rows_of = scratch.rearrange("a (j r) t n -> a (r t) j n", j=NG)
                sp.dma_start(q_stack[u][:, :, :].bitcast(F32), rows_of[0]).then_inc(stacked[n % 2], 16)
                for i in range(GH):
                    strip = slice(32 * i, 32 * (i + 1))
                    sp.dma_start(k_stack[u][strip, :, i, :].bitcast(F32), rows_of[1, strip]).then_inc(stacked[n % 2], 16)

            for _, (_, u, kind, arg, _) in ORDER["sp"]:
                if kind == "qk":
                    stack(u, arg)
                if kind == "leave":
                    sp.wait_ge(y_ready, u + 1)
                    sp.dma_start(out.rearrange("b t d -> t b d")[:, u * S:(u + 1) * S, :],
                                 y_tok[:, u * S:(u + 1) * S, :]).then_inc(stored, 16)
            sp.wait_ge(stored, 16 * U)

        @block.gpsimd
        def _(pool):
            pool.dma_start(rows[:, :, :, :].rearrange("p a o d -> p (a o d)"), rows_in.partition_broadcast(128)).then_inc(row_loaded, 16)
            pool.dma_start(mask_i[:, :, :].rearrange("p b t -> p (b t)"), mask_in.partition_broadcast(128)).then_inc(row_loaded, 16)

            def power(u, which):
                pool.wait_ge(var_ready[u], NO[which] + 1)
                nc.gpsimd.tensor_tensor(rstd[:, u, :], base[:, u, :], minus_half, ALU.pow).then_inc(rstd_ready[u], 1)

            def split(step):
                _, u, _, layer, (b,) = step
                n = U * att_no(layer) + u
                if n >= 2:
                    pool.wait_ge(parts_stored[n % 2], PARTS * (n // 2))
                wait_done(pool, step, b)
                both = qkT[u][:, :, :, :].rearrange("p a s t -> p a (s t)")
                nc.gpsimd.tensor_scalar(qk_high[u][:, :, :], both, 1.0, None, ALU.mult).then_inc(split_high, 1)
                pool.wait_ge(split_high, n + 1)
                nc.gpsimd.tensor_tensor(qk_low[u][:, :, :], both, qk_high[u][:, :, :].bitcast(F32), ALU.subtract)\
                    .then_inc(split_low, 1)

            def clear_stack(u):
                nc.gpsimd.memset(k_stack[u][:, :, :, :].bitcast(F32), 0.0).then_inc(stack_cleared, 1)

            clear_stack(0)
            pool.wait_ge(const_loaded, 16)
            for _, step in ORDER["pool"]:
                if step[2] == "stats":
                    power(step[1], step[3])
                if step[2] == "lin_y":
                    power(step[1], "1s")
                if step[2] == "qk":
                    split(step)
                    if step[1:4] == (0, "qk", 0):
                        clear_stack(1)

        @block.scalar
        def _(act):
            cols = slice(WCOL[LOADS[0][0]].start, WCOL[LOADS[0][-1]].stop)
            act.dma_start(w[:, cols], w_in[:, cols]).then_inc(w_loaded[0], 16)
            act.dma_start(const[:, :], const_in).then_inc(const_loaded, 16)
            for i in range(2, len(LOADS), 2):
                cols = slice(WCOL[LOADS[i][0]].start, WCOL[LOADS[i][-1]].stop)
                act.dma_start(w[:, cols], w_in[:, cols]).then_inc(w_loaded[i], 16)
            act.wait_ge(vec_loaded, 16)
            nc.scalar.activation(c_tanh[:, :], vec[:, VCOL["c"]], ACT.Tanh, scale=0.5).then_inc(c_tanh_ready, 1)

            def exps(g):
                act.wait_ge(max_ready, g + 1)
                if g >= 4:
                    act.wait_ge(turned_ready, g - 3)
                for i in range(GH):
                    last = nc.scalar.activation(probs[:, g % 4, i, :], ps_scores[g % NSC][:, i * T:(i + 1) * T], ACT.Exp,
                                                bias=neg_max[:, g, i:i + 1],
                                                accum_out=den[:, g // NG, GH * (g % NG) + i:GH * (g % NG) + i + 1])
                last.then_inc(probs_ready, 1)

            def inverse_sums(q):
                act.wait_ge(att_ready, q + 1)
                nc.scalar.activation(rdenT[:, q % 2, :], ps_att[:, T:2 * T], ACT.Copy).then_inc(rdenT_ready, 1)

            def dense(step):
                _, u, kind, arg, banks = step
                ps = [ps_dense[b] for b in banks]
                if kind == "enter":
                    wait_filled(act, step, banks[0])
                    nc.scalar.activation(xT[u][:, :, :], by_seq(ps[0][:, 0:N]), ACT.Copy).then_inc(x_ready[u], 1)
                if kind == "turned":
                    wait_filled(act, step, banks[0])
                    act.wait_ge(cond_ready, {"0": 1, "1": 2, "2": 4, "3": 5}[arg[0]])
                    for s in range(S):
                        i = S * u + s
                        last = nc.scalar.activation(hT[u][:, s, :], ps[0][:, s * T:(s + 1) * T], ACT.Identity,
                                                    scale=mod_a[:, NO[arg], i:i + 1], bias=mod_b[:, NO[arg], i:i + 1])
                    last.then_inc(drained[banks[0]], 1)
                    if arg == "1s":
                        wait_done(act, step, banks[0])
                        nc.scalar.activation(l_t[u][:, :, :], hT[u][:, :, :], ACT.Tanh).then_inc(lin_tanh[u], 1)
                if kind == "qk":
                    n = U * att_no(arg) + u
                    if n >= 2:
                        act.wait_ge(split_low, n - 1)
                    wait_filled(act, step, banks[0])
                    q, k = by_seq(ps[0][:, 0:N]), by_seq(ps[0][:, N:2 * N])
                    if arg == 2:
                        nc.scalar.activation(qkT[u][:, 0, :, :], q, ACT.Identity, scale=HD ** -0.5, bias=bq2_scaled[:, :])
                        last = nc.scalar.activation(qkT[u][:, 1, :, :], k, ACT.Identity, bias=vcol("bk2"))
                    else:
                        nc.scalar.activation(qkT[u][:, 0, :, :], q, ACT.Copy, scale=HD ** -0.5)
                        last = nc.scalar.activation(qkT[u][:, 1, :, :], k, ACT.Copy)
                    last.then_inc(drained[banks[0]], 1)
                if kind == "up":
                    for h in range(2):
                        wait_filled(act, step, banks[h])
                        for c in (2 * h, 2 * h + 1):
                            last = nc.scalar.activation(hid[u][:, c, :], ps[h][:, (c % 2) * N:(c % 2 + 1) * N], ACT.Gelu,
                                                        bias=vcol(f"bup{arg}", c))
                        last.then_inc(drained[banks[h]], 1)
                if kind == "gated":
                    n = gated_no[step]
                    wait_filled(act, step, banks[0])
                    if n >= 2:
                        prev = list(gated_no)[n - 2]
                        wait_done(act, prev, prev[4][0])
                    nc.scalar.activation(th[:, n % 2, :], ps[0][:, 0:N], ACT.Tanh, scale=0.5, bias=bup3_half[:, arg:arg + 1])
                    nc.scalar.activation(half[:, n % 2, :], ps[0][:, 0:N], ACT.Identity, scale=0.5,
                                         bias=bup3_half[:, arg:arg + 1]).then_inc(gate_halves, 1)
                if kind == "lin_qk":
                    act.wait_ge(lin_sub[u], 1)
                    nc.scalar.activation(l_e[u][:, 0, :, :], l_qs[u][:, :, :], ACT.Exp)
                    for s in range(S):
                        last = nc.scalar.activation(l_e[u][:, 1, s, :], l_k[u][:, s, :], ACT.Exp, bias=k_max[:, u, s:s + 1],
                                                    accum_out=k_sum[:, u, s:s + 1])
                    last.then_inc(lin_exp[u], 1)
                if kind == "lin_turn":
                    wait_filled(act, step, banks[0])
                    nc.scalar.activation(l_eT[u][:, :], ps[0][:, :], ACT.Copy).then_inc(drained[banks[0]], 1)
                if kind == "leave":
                    wait_filled(act, step, banks[0])
                    nc.scalar.activation(y_tok[:, u * S:(u + 1) * S, :], by_seq(ps[0][:, 0:N]), ACT.Copy).then_inc(y_ready, 1)

            for what, which in ORDER["act"]:
                if what == "exps":
                    exps(which)
                elif what == "inverse_sums":
                    inverse_sums(which)
                else:
                    dense(which)

        @block.vector
        def _(dve):
            own = [0]

            def link(ins):
                own[0] += 1
                ins.then_inc(dve_own, 1)
                dve.wait_ge(dve_own, own[0])

            dve.wait_ge(vec_loaded, 16)
            link(nc.vector.tensor_scalar(c_half[:, :], vec[:, VCOL["c"]], 0.5, None, ALU.mult))
            dve.wait_ge(c_tanh_ready, 1)
            nc.vector.scalar_tensor_tensor(sil[:, :], c_tanh[:, :], 1.0, c_half[:, :], ALU.add, ALU.mult).then_inc(silu_ready, 1)
            nc.vector.tensor_scalar(bq2_scaled[:, :], vcol("bq2"), HD ** -0.5, None, ALU.mult)
            nc.vector.tensor_scalar(bup3_half[:, :], vec[:, VCOL["bup3"].start:VCOL["bup3"].start + FC], 0.5, None, ALU.mult)

            def maxima(g):
                dve.wait_ge(scores_ready, g + 1)
                nc.vector.tensor_reduce(neg_max[:, g, :], ps_scores[g % NSC][:, :].rearrange("p (h k) -> p h k", h=GH), AX.X,
                                        ALU.max, negate=True).then_inc(max_ready, 1)

            def turned_out(g):
                dve.wait_ge(turned_ready, g + 1)
                q = g // NG
                if q >= 2 and g % NG == 0:
                    dve.wait_ge(att_ready, q - 1)
                nc.vector.tensor_copy(probsT[:, q % 2, GH * (g % NG):GH * (g % NG + 1), :].rearrange("p h t -> p (h t)"),
                                      ps_turned[g % NTU][:, :]).then_inc(turned_read, 1)

            def inverse(q):
                dve.wait_ge(probs_ready, NG * (q + 1))
                link(nc.vector.reciprocal(rden[:, q, :, 0], den[:, q, :]))
                if q >= 2:
                    dve.wait_ge(att_ready, q - 1)
                nc.vector.tensor_copy(rden_wide[:, q % 2, :, :], rden[:, q, :, :].broadcast_to([128, H, HD])).then_inc(rden_ready, 1)

            def normalise(q):
                _, u, s, _ = group(q * NG)
                dve.wait_ge(rdenT_ready, q + 1)
                nc.vector.tensor_tensor(att[u][:, s, :], ps_att[:, 0:T], rdenT[:, q % 2, :], ALU.mult).then_inc(att_read, 1)

            def statistics(u, which, src):
                for s in range(S):
                    last = nc.vector.bn_stats(bn[:, u, s, :], src(s))
                link(last)
                for s in range(S):
                    last = nc.vector.bn_aggr(mv[:, u, s, :], bn[:, u, s, :])
                link(last)
                if which[0] == "3":
                    link(nc.vector.tensor_tensor(base[:, u, :], mv[:, u, :, 0], mv[:, u, :, 0], ALU.mult))
                    link(nc.vector.tensor_tensor(base[:, u, :], base[:, u, :], mv[:, u, :, 1], ALU.add))
                    nc.vector.tensor_scalar(base[:, u, :], base[:, u, :], EPS3 * EPS3, None, ALU.max).then_inc(var_ready[u], 1)
                else:
                    nc.vector.tensor_scalar(base[:, u, :], mv[:, u, :, 1], EPS, None, ALU.add).then_inc(var_ready[u], 1)

            def row_source(u, which):
                if which == "0a":
                    return lambda s: x_tok[:, S * u + s, :]
                if which == "1s":
                    return lambda s: l_y[u][:, s, :]
                (b,) = step_of[u, "stats", which][4]
                return lambda s: ps_dense[b][:, s * T:(s + 1) * T]

            def add_scaled(step, name, gate):
                _, u, _, _, (b,) = step
                for s in range(S):
                    last = nc.vector.tensor_scalar(scaled[u][:, s, :], ps_dense[b][:, s * T:(s + 1) * T], vcol(name),
                                                   gate(S * u + s), ALU.add, ALU.mult)
                link(last)
                nc.vector.tensor_tensor(xT[u][:, :, :], xT[u][:, :, :], scaled[u][:, :, :], ALU.add).then_inc(x_ready[u], 1)

            def condition(step):
                _, _, _, arg, (b,) = step
                wait_filled(dve, step, b)
                ps = ps_dense[b]

                def plus_bias(first, n, name):
                    nc.vector.tensor_tensor(cnd[:, first:first + n, :], ps[:, 0:n * B].rearrange("p (i b) -> p i b", i=n),
                                            vec[:, VCOL[name]].rearrange("p (i o) -> p i o", o=1).broadcast_to([128, n, B]),
                                            ALU.add).then_inc(drained[b], 1)
                    wait_done(dve, step, b)

                def modulate(which, scale, shift, g, bias):
                    nc.vector.tensor_scalar(mod_a[:, NO[which], :], cnd[:, scale, :], 1.0, vcol(g), ALU.add, ALU.mult)
                    link(nc.vector.tensor_scalar(tmp[:, 0, :], cnd[:, scale, :], 1.0, vcol(bias), ALU.add, ALU.mult))
                    return nc.vector.tensor_tensor(mod_b[:, NO[which], :], tmp[:, 0, :], cnd[:, shift, :], ALU.add)

                if arg == "0":
                    plus_bias(0, 6, "bc0")
                    for which, i in (("0a", 0), ("0m", 3)):
                        nc.vector.tensor_scalar(mod_a[:, NO[which], :], cnd[:, i + 1, :], 1.0, None, ALU.add)
                        last = nc.vector.tensor_copy(mod_b[:, NO[which], :], cnd[:, i, :])
                    last.then_inc(cond_ready, 1)
                if arg == "1":
                    plus_bias(6, 2, "bcond1")
                    nc.vector.tensor_copy(mod_a[:, NO["1a"], :], vcol("g1").broadcast_to([128, B]))
                    nc.vector.tensor_copy(mod_b[:, NO["1a"], :], vcol("b1").broadcast_to([128, B]))
                    link(modulate("1s", 6, 7, "gs1", "bs1"))
                    for m in (mod_a, mod_b):
                        last = nc.vector.tensor_scalar(m[:, NO["1s"], :], m[:, NO["1s"], :], 0.5, None, ALU.mult)
                    last.then_inc(cond_ready, 1)
                if arg == "2a":
                    nc.vector.tensor_tensor(bo2_full[:, :], ps[:, 2 * B:2 * B + 1], vcol("bo2"), ALU.add)
                    plus_bias(8, 2, "bcond2a")
                    modulate("2a", 9, 8, "g2a", "b2a").then_inc(cond_ready, 1)
                if arg == "2m":
                    plus_bias(10, 2, "bcond2m")
                    modulate("2m", 11, 10, "g2m", "b2m").then_inc(cond_ready, 1)
                if arg == "3":
                    plus_bias(12, 2, "bcond3")
                    link(nc.vector.tensor_scalar(tmp[:, 1, :], cnd[:, 12, :], 1.0, 0.1, ALU.add, ALU.max))
                    for which in ("3a", "3m"):
                        nc.vector.tensor_scalar(mod_a[:, NO[which], :], tmp[:, 1, :], 10.0, vcol("g3"), ALU.min, ALU.mult)
                        last = nc.vector.tensor_copy(mod_b[:, NO[which], :], cnd[:, 13, :])
                    last.then_inc(cond_ready, 1)
                    dve.wait_ge(row_loaded, 32)
                    nc.vector.tensor_scalar(masked[:, :, 0, :], mask_i[:, :, :], 0.0, MASKED, ALU.is_equal, ALU.mult)\
                        .then_inc(mask_ready, 1)

            def dense(step):
                _, u, kind, arg, banks = step
                b = banks[0] if banks else None
                ps = ps_dense[b] if banks else None
                if kind == "cond":
                    condition(step)
                if kind == "enter":
                    nc.vector.memset(v_pad[u][:, :, :, :], 0.0).then_inc(v_cleared, 1)
                if kind == "stats":
                    if arg == "0a":
                        dve.wait_ge(x_loaded, 16)
                    else:
                        wait_filled(dve, step, b)
                    statistics(u, arg, row_source(u, arg))
                if kind == "normed":
                    src = row_source(u, arg)
                    dve.wait_ge(rstd_ready[u], NO[arg] + 1)
                    for s in range(S):
                        if arg[0] == "3":
                            last = nc.vector.tensor_scalar(xhat[u][:, s, :], src(s), rstd[:, u, s:s + 1], None, ALU.mult)
                        else:
                            last = nc.vector.tensor_scalar(xhat[u][:, s, :], src(s), mv[:, u, s, 0:1], rstd[:, u, s:s + 1],
                                                           ALU.subtract, ALU.mult)
                    if arg in ("0a", "1s"):
                        last.then_inc(xhat_ready[u], 1)
                    else:
                        last.then_inc(drained[step_of[u, "stats", arg][4][0]], 1)
                if kind == "v":
                    wait_filled(dve, step, b)
                    if arg == 0:
                        dve.wait_ge(v_cleared, u + 1)
                    for s in range(S):
                        dst = v_pad[u][:, s, :, :].rearrange("p (j i) c -> p j (i c)", i=GH)
                        dst = bass.AP(dst.tensor, dst.offset, [dst.ap[0], [GH * 32, NG], [32 + HD, GH], [1, HD]])
                        last = nc.vector.tensor_copy(dst, ps[:, s * D:(s + 1) * D].rearrange("p (j i d) -> p j i d", j=NG, i=GH))
                    last.then_inc(drained[b], 1)
                if kind == "out" and arg == 0:
                    wait_filled(dve, step, b)
                    for s in range(S):
                        last = nc.vector.scalar_tensor_tensor(xT[u][:, s, :], ps[:, s * T:(s + 1) * T], cnd[:, 2, S * u + s:S * u + s + 1],
                                                              xT[u][:, s, :], ALU.mult, ALU.add)
                    last.then_inc(x_ready[u], 1)
                if (kind == "out" and arg) or (kind == "down" and arg):
                    wait_filled(dve, step, b)
                    bias = {("out", 2): bo2_full[:, :], ("out", 3): vcol("bo3"), ("down", 2): vcol("bdown2"),
                            ("down", 3): vcol("bdown3")}[kind, arg]
                    nc.vector.scalar_tensor_tensor(xT[u][:, :, :], by_seq(ps[:, 0:N]), bias, xT[u][:, :, :], ALU.add, ALU.add)\
                        .then_inc(x_ready[u], 1)
                if kind == "down" and arg == 0:
                    wait_filled(dve, step, b)
                    add_scaled(step, "bdown0", lambda i: cnd[:, 5, i:i + 1])
                if kind == "lin_out":
                    wait_filled(dve, step, b)
                    add_scaled(step, "bo1", lambda i: vec[:, VCOL["c"].start + i:VCOL["c"].start + i + 1])
                if kind == "gated":
                    n = gated_no[step]
                    dve.wait_ge(gate_halves, n + 1)
                    link(nc.vector.scalar_tensor_tensor(silu_g[:, n % 2, :], th[:, n % 2, :], 1.0, half[:, n % 2, :], ALU.add, ALU.mult))
                    nc.vector.scalar_tensor_tensor(hid[u][:, arg, :], ps[:, N:2 * N], vcol("bup3", FC + arg), silu_g[:, n % 2, :],
                                                   ALU.add, ALU.mult).then_inc(drained[b], 1)
                if kind == "lin_qk":
                    wait_filled(dve, step, b)
                    dve.wait_ge(row_loaded, 32)
                    nc.vector.tensor_tensor(l_q[u][:, :, :], by_seq(ps[:, 0:N]), rows[:, 0, :, :].broadcast_to([128, S, D]), ALU.add)
                    nc.vector.tensor_scalar(l_k[u][:, :, :], by_seq(ps[:, N:2 * N]), vcol("bk1"), None, ALU.add).then_inc(drained[b], 1)
                    wait_done(dve, step, b)
                    heads = l_q[u][:, :, :].rearrange("p s (h d) -> p (s h) d", d=HD)
                    nc.vector.tensor_reduce(k_max[:, u, :], l_k[u][:, :, :], AX.X, ALU.max, negate=True)
                    link(nc.vector.tensor_reduce(q_max[:, u, :], heads, AX.X, ALU.max, negate=True))
                    nc.vector.tensor_tensor(l_qs[u][:, :, :].rearrange("p s (h d) -> p (s h) d", d=HD), heads,
                                            q_max[:, u, :].rearrange("p (h o) -> p h o", o=1).broadcast_to([128, S * H, HD]),
                                            ALU.add).then_inc(lin_sub[u], 1)
                if kind == "lin_v":
                    wait_filled(dve, step, b)
                    nc.vector.tensor_tensor(l_v[u][:, :, :], by_seq(ps[:, 0:N]), rows[:, 1, :, :].broadcast_to([128, S, D]), ALU.add)\
                        .then_inc(drained[b], 1)
                if kind == "lin_turn":
                    dve.wait_ge(lin_exp[u], 1)
                    link(nc.vector.tensor_reduce(q_sum[:, u, :], l_e[u][:, 0, :, :].rearrange("p s (h d) -> p (s h) d", d=HD), AX.X, ALU.add))
                    nc.vector.reciprocal(q_inv[:, u, :], q_sum[:, u, :])
                    link(nc.vector.reciprocal(k_inv[:, u, :], k_sum[:, u, :]))
                if kind == "lin_ctx":
                    wait_filled(dve, step, b)
                    for s in range(S):
                        last = nc.vector.scalar_tensor_tensor(l_ctx[u][:, s, :], ps[:, s * D:(s + 1) * D], k_inv[:, u, s:s + 1], blocks,
                                                              ALU.mult, ALU.mult)
                    last.then_inc(drained[b], 1)
                if kind == "lin_y":
                    wait_filled(dve, step, b)
                    nc.vector.tensor_tensor(l_y[u][:, :, :].rearrange("p s (h d) -> p (s h) d", d=HD),
                                            ps[:, 0:N].rearrange("p (h d) -> p h d", d=HD),
                                            q_inv[:, u, :].rearrange("p (h o) -> p h o", o=1).broadcast_to([128, S * H, HD]),
                                            ALU.mult).then_inc(drained[b], 1)
                    wait_done(dve, step, b)
                    statistics(u, "1s", row_source(u, "1s"))
                if kind == "turned" and arg == "1s":
                    dve.wait_ge(lin_tanh[u], 1)
                    nc.vector.scalar_tensor_tensor(l_hs[u][:, :, :], l_t[u][:, :, :], 1.0, hT[u][:, :, :], ALU.add, ALU.mult)\
                        .then_inc(lin_silu[u], 1)

            for what, which in ORDER["dve"]:
                if what == "maxima":
                    maxima(which)
                elif what == "turned_out":
                    turned_out(which)
                elif what == "inverse":
                    inverse(which)
                elif what == "normalise":
                    normalise(which)
                else:
                    dense(which)

        @block.tensor
        def _(pe):
            def scores(g):
                layer, u, s, j = group(g)
                if j == 0 and s == 0:
                    pe.wait_ge(stacked[u % 2], STACKING * ((U * att_no(layer) + u) // 2 + 1))
                if g >= NSC:
                    pe.wait_ge(probs_ready, g - NSC + 1)
                ps = ps_scores[g % NSC]
                last = nc.tensor.matmul(ps[:, :], q_stack[u][:, j, s * T:(s + 1) * T], k_stack[u][:, j, :, s * T:(s + 1) * T],
                                        start=True, stop=True)
                last.then_inc(scores_ready, 1)

            def turn(g):
                pe.wait_ge(probs_ready, g + 1)
                if g >= NTU:
                    pe.wait_ge(turned_read, g - NTU + 1)
                for i in range(GH):
                    last = nc.tensor.transpose(ps_turned[g % NTU][:, i * T:(i + 1) * T], probs[:, g % 4, i, :], ident)
                last.then_inc(turned_ready, 1)

            def values(q):
                layer, u, s, _ = group(q * NG)
                pe.wait_ge(turned_read, NG * (q + 1))
                wait_written(pe, u, "v", layer)
                if q >= 1:
                    pe.wait_ge(att_read, q)
                for i in range(GH):
                    for j in range(NG):
                        h = GH * j + i
                        nc.tensor.matmul(ps_att[32 * j:32 * j + 32, 0:T], v_pad[u][:, s, h, :], probsT[:, q % 2, h, :],
                                         start=i == 0, stop=i == GH - 1)
                pe.wait_ge(rden_ready, q + 1)
                nc.tensor.transpose(ps_att[:, T:2 * T], rden_wide[:, q % 2, :, :].rearrange("p h d -> p (h d)"), ident)\
                    .then_inc(att_ready, 1)

            def dense(step):
                _, u, kind, arg, banks = step
                for b in banks:
                    wait_free(pe, step, b)
                b = banks[0] if banks else None
                ps = ps_dense[b] if banks else None
                flat = lambda tile: tile.rearrange("p s t -> p (s t)")
                h_flat = flat(hT[u][:, :, :])

                def mm(out, lhsT, rhs, start=True, stop=True):
                    return nc.tensor.matmul(out, lhsT, rhs, start=start, stop=stop)

                if kind == "cond":
                    pe.wait_ge(silu_ready, 1)
                    name = f"cond{arg}"
                    wait_weights(pe, name)
                    rhs = vec[:, VCOL["c"]] if arg[0] == "2" else sil[:, :]
                    for i in range(6 if arg == "0" else 2):
                        last = mm(ps[:, i * B:(i + 1) * B], wcol(name, i), rhs)
                    if arg == "2a":
                        last = mm(ps[:, 2 * B:2 * B + 1], wcol("o2"), vcol("bv2"))
                    last.then_inc(filled[b], 1)
                if kind == "enter":
                    pe.wait_ge(x_loaded, 16)
                    pe.wait_ge(const_loaded, 16)
                    for s in range(S):
                        last = nc.tensor.transpose(ps[:, s * T:(s + 1) * T], x_tok[:, S * u + s, :], ident)
                    last.then_inc(filled[b], 1)
                if kind == "stats" and banks:
                    pe.wait_ge(x_ready[u], BEFORE_NORM[arg])
                    for s in range(S):
                        last = nc.tensor.transpose(ps[:, s * T:(s + 1) * T], xT[u][:, s, :], ident)
                    last.then_inc(filled[b], 1)
                if kind == "turned":
                    if arg in ("0a", "1s"):
                        pe.wait_ge(xhat_ready[u], 1 if arg == "0a" else 2)
                    else:
                        wait_written(pe, u, "stats", arg)
                    for s in range(S):
                        last = nc.tensor.transpose(ps[:, s * T:(s + 1) * T], xhat[u][:, s, :], ident)
                    last.then_inc(filled[b], 1)
                if kind == "qk":
                    wait_written(pe, u, "turned", f"{arg}a")
                    wait_weights(pe, f"q{arg}")
                    mm(ps[:, 0:N], wcol(f"q{arg}"), h_flat)
                    mm(ps[:, N:2 * N], wcol(f"k{arg}"), h_flat).then_inc(filled[b], 1)
                if kind in ("v", "lin_v"):
                    wait_written(pe, u, "turned", f"{arg}a")
                    wait_weights(pe, f"v{arg}")
                    for s in range(S):
                        last = mm(ps[:, s * D:(s + 1) * D], hT[u][:, s, :], wcol(f"v{arg}"))
                    last.then_inc(filled[b], 1)
                if kind == "out":
                    pe.wait_ge(att_read, B * att_no(arg) + S * (u + 1))
                    wait_weights(pe, f"o{arg}")
                    mm(ps[:, 0:N], wcol(f"o{arg}"), flat(att[u][:, :, :])).then_inc(filled[b], 1)
                if kind == "up":
                    wait_written(pe, u, "turned", f"{arg}m")
                    wait_weights(pe, f"up{arg}")
                    for c in range(FC):
                        last = mm(ps_dense[banks[c // 2]][:, (c % 2) * N:(c % 2 + 1) * N], wcol(f"up{arg}", c), h_flat)
                        if c % 2:
                            last.then_inc(filled[banks[c // 2]], 1)
                if kind == "gated":
                    wait_written(pe, u, "turned", "3m")
                    wait_weights(pe, "up3")
                    mm(ps[:, 0:N], wcol("up3", arg), h_flat)
                    mm(ps[:, N:2 * N], wcol("up3", FC + arg), h_flat).then_inc(filled[b], 1)
                if kind == "down":
                    if arg == 3:
                        for c in range(FC):
                            wait_written(pe, u, "gated", c)
                    else:
                        wait_written(pe, u, "up", arg)
                    for c in range(FC):
                        last = mm(ps[:, 0:N], wcol(f"down{arg}", c), hid[u][:, c, :], start=c == 0, stop=c == FC - 1)
                    last.then_inc(filled[b], 1)
                if kind == "lin_qk":
                    wait_written(pe, u, "turned", "1a")
                    wait_weights(pe, "q1")
                    for s in range(S):
                        mm(ps[:, s * D:(s + 1) * D], hT[u][:, s, :], wcol("q1"))
                    mm(ps[:, N:2 * N], wcol("k1"), h_flat).then_inc(filled[b], 1)
                if kind == "lin_turn":
                    pe.wait_ge(lin_exp[u], 1)
                    for i in range(2 * S):
                        last = nc.tensor.transpose(ps[:, i * T:(i + 1) * T], l_e[u][:, i // S, i % S, :], ident)
                    last.then_inc(filled[b], 1)
                if kind == "lin_ctx":
                    wait_written(pe, u, "lin_turn", 1)
                    wait_written(pe, u, "lin_v", 1)
                    for s in range(S):
                        last = mm(ps[:, s * D:(s + 1) * D], l_eT[u][:, (S + s) * T:(S + s + 1) * T], l_v[u][:, s, :])
                    last.then_inc(filled[b], 1)
                if kind == "lin_y":
                    wait_written(pe, u, "lin_ctx", 1)
                    for s in range(S):
                        last = mm(ps[:, s * D:(s + 1) * D], l_eT[u][:, s * T:(s + 1) * T], l_ctx[u][:, s, :])
                    last.then_inc(filled[b], 1)
                if kind == "lin_out":
                    pe.wait_ge(lin_silu[u], 1)
                    mm(ps[:, 0:N], wcol("o1"), flat(l_hs[u][:, :, :])).then_inc(filled[b], 1)
                if kind == "leave":
                    pe.wait_ge(x_ready[u], len(SUMS))
                    for s in range(S):
                        last = nc.tensor.transpose(ps[:, s * T:(s + 1) * T], xT[u][:, s, :], ident)
                    last.then_inc(filled[b], 1)

            for what, which in ORDER["pe"]:
                if what == "scores":
                    scores(which)
                elif what == "turn":
                    turn(which)
                elif what == "values":
                    values(which)
                else:
                    dense(which)


def kernel(**inputs):
    import numpy as np
    import concourse.bacc as bacc
    from concourse.bass_utils import run_bass_kernel_spmd

    def arr(name):
        return np.asarray(inputs[name])

    def cols(name):
        return arr(name).reshape(-1, 128).T

    def chunked(m):
        return m.reshape(-1, 128, m.shape[1]).transpose(1, 0, 2).reshape(128, -1)

    def per_query_head(m):
        return np.repeat(m.reshape(HD // 2, HD, D), GH, axis=0).reshape(D, D)

    qkv3 = arr("L3_cond_qkv_w")
    weights = {
        "cond0": arr("L0_cond_wc").T, "q0": arr("L0_cond_wq").T, "k0": per_query_head(arr("L0_cond_wk")).T,
        "v0": per_query_head(arr("L0_cond_wv")).T, "o0": arr("L0_cond_wo").T, "up0": arr("L0_cond_w1").T,
        "down0": chunked(arr("L0_cond_w2").T),
        "cond1": arr("L1_cond_emb_W"), "q1": arr("L1_cond_Wq"), "k1": arr("L1_cond_Wk"), "v1": arr("L1_cond_Wv"),
        "o1": arr("L1_cond_out_W"),
        "cond2a": arr("L2_cond_wt_attn"), "cond2m": arr("L2_cond_wt_ffn"), "q2": arr("L2_cond_wq"), "k2": arr("L2_cond_wk"),
        "v2": arr("L2_cond_wv"), "o2": arr("L2_cond_wo"), "up2": arr("L2_cond_w1"), "down2": chunked(arr("L2_cond_w2")),
        "cond3": np.concatenate([arr("L3_cond_scale_w").T, arr("L3_cond_shift_w").T], axis=1),
        "q3": qkv3[0:D].T, "k3": qkv3[D:2 * D].T, "v3": qkv3[2 * D:].T, "o3": arr("L3_cond_proj_w").T,
        "up3": arr("L3_cond_mlp_w1").T, "down3": chunked(arr("L3_cond_mlp_w2").T),
    }
    vectors = {
        "c": arr("cond_1024").T, "bc0": cols("L0_cond_bc"), "bup0": cols("L0_cond_b1"), "bdown0": cols("L0_cond_b2"),
        "g1": cols("L1_cond_norm_g"), "b1": cols("L1_cond_norm_b"), "bk1": cols("L1_cond_bk"), "bcond1": cols("L1_cond_emb_b"),
        "gs1": cols("L1_cond_sn_g"), "bs1": cols("L1_cond_sn_b"), "bo1": cols("L1_cond_out_b"),
        "g2a": cols("L2_cond_ln1_w"), "b2a": cols("L2_cond_ln1_b"), "g2m": cols("L2_cond_ln2_w"), "b2m": cols("L2_cond_ln2_b"),
        "bq2": cols("L2_cond_bq"), "bk2": cols("L2_cond_bk"), "bv2": cols("L2_cond_bv"), "bo2": cols("L2_cond_bo"),
        "bcond2a": cols("L2_cond_bt_attn"), "bcond2m": cols("L2_cond_bt_ffn"), "bup2": cols("L2_cond_b1"),
        "bdown2": cols("L2_cond_b2"), "g3": cols("L3_cond_norm_w"),
        "bcond3": np.concatenate([cols("L3_cond_scale_b"), cols("L3_cond_shift_b")], axis=1),
        "bo3": cols("L3_cond_proj_b"), "bup3": cols("L3_cond_mlp_b1"), "bdown3": cols("L3_cond_mlp_b2"),
    }
    head = np.arange(D) // HD
    const = np.concatenate([
        np.eye(D), head[:, None] == head[None, :], np.full((D, S), -0.5),
    ], axis=1).astype(np.float32)
    arrays = {
        "x": np.ascontiguousarray(arr("x")),
        "vectors": np.ascontiguousarray(np.concatenate([vectors[n] for n, _ in VECTORS], axis=1)),
        "weights": np.ascontiguousarray(np.concatenate([weights[n] for n, _ in WEIGHTS], axis=1)),
        "row_biases": np.concatenate([arr("L1_cond_bq"), arr("L1_cond_bv")]),
        "mask": np.ascontiguousarray(arr("mask_BxS_ik0")).reshape(-1),
        "constants": const,
        "pads": np.stack([np.repeat(np.arange(D)[:, None] % HD == 0, N, axis=1), np.zeros((D, N))]).astype(np.float32),
    }
    nc = bacc.Bacc("TRN2", target_bir_lowering=False, num_devices=1)
    args = [nc.dram_tensor(n, a.shape, mybir.dt.from_np(a.dtype), kind="ExternalInput").ap() for n, a in arrays.items()]
    out = nc.dram_tensor("out", (B, T, D), F32, kind="ExternalOutput").ap()
    parts = nc.dram_tensor("parts", (2, 2, D, ROWS, N), F32, kind="Internal").ap()
    build(nc, *args, parts, out)
    r = run_bass_kernel_spmd(nc, [arrays], core_ids=[0])
    return r.results[0]["out"]
```
